# Optimizing a Trainium2 kernel written in Bass

```python
import numpy as np
import jax
import jax.numpy as jnp

def _softmax(x, axis=-1):
    return jax.nn.softmax(x, axis=axis)

def _gelu(x):
    return jax.nn.gelu(x, approximate=True)

def _silu(x):
    return jax.nn.silu(x)

def _sigmoid(x):
    return jax.nn.sigmoid(x)

def _layernorm(x, axis=-1, eps=1e-05):
    m = jnp.mean(x, axis=axis, keepdims=True)
    v = jnp.var(x, axis=axis, keepdims=True)
    return (x - m) / jnp.sqrt(v + eps)

def _scatter_add(tgt, idx, src, axis=0):
    return tgt.at[idx].add(src)

def _segment_sum(src, seg, n):
    return jax.ops.segment_sum(src, seg, n)
kernel_name = 'mk_xattn_ffn_d2_seqx_r4_e722a4'

def setup_inputs(seed: int=0):
    np.random.seed(seed)
    _w = jnp.asarray

    def _rec_inputs():
        import jax
        import jax.numpy as jnp
        _rk = jax.random.key(seed)
        x = 7.22e-05 + 1 * jax.random.normal(jax.random.fold_in(_rk, 1), (4, 512, 512), jnp.float32)
        _lenS = 512 - jax.random.randint(jax.random.fold_in(_rk, 7), (4,), 0, max(1, 512 // 4) + 1, jnp.int32)
        _lenS2 = 512 - jax.random.randint(jax.random.fold_in(_rk, 8), (4,), 0, max(1, 512 // 4) + 1, jnp.int32)
        _ctx_1024P = jax.random.normal(jax.random.fold_in(_rk, 11), (4, 16, 256), jnp.float32)
        _ctx_1024c = jax.random.dirichlet(jax.random.fold_in(_rk, 511), 0.3 * jnp.ones((16,), jnp.float32), (4, 512))
        _ctx_1024t = jnp.einsum('bsk,bkd->bsd', _ctx_1024c, _ctx_1024P)
        _ctx_1024t = _ctx_1024t * jax.lax.rsqrt(jnp.mean(jnp.square(_ctx_1024t)) + 1e-12) * 0.953939
        ctx_1024 = 2.81802e-05 + 1.00001 * (_ctx_1024t + 0.3 * jax.random.normal(jax.random.fold_in(_rk, 611), (4, 512, 256), jnp.float32))
        fside_BxSx2_0 = jax.random.uniform(jax.random.fold_in(_rk, 12), (4, 512, 2), jnp.float32, 0.0, 0.999707)
        return (x, ctx_1024, fside_BxSx2_0)
    x, ctx_1024, fside_BxSx2_0 = _rec_inputs()

    def _L0_xattn_setup():
        import jax, jax.numpy as jnp
        import numpy as np
        key = jax.random.key(seed)
        ks = jax.random.split(key, 6)
        B, L, N, C, D = (8, 128, 512, 256, 128)
        return {'teacher_logits': jax.random.normal(ks[0], (B, L, N), dtype=jnp.float32), 'teacher_features': jax.random.normal(ks[1], (B, N, C), dtype=jnp.float32), 'Wq': jax.random.normal(ks[2], (D, C), dtype=jnp.float32) * (1.0 / np.sqrt(C)), 'bq': jnp.zeros((D,), dtype=jnp.float32), 'Wk': jax.random.normal(ks[3], (D, C), dtype=jnp.float32) * (1.0 / np.sqrt(C)), 'bk': jnp.zeros((D,), dtype=jnp.float32)}
    _L0_xattn_all = _L0_xattn_setup()
    _L0_xattn_in = {k: v for k, v in _L0_xattn_all.items() if k in ('Wq', 'bq', 'Wk', 'bk')}
    del _L0_xattn_all

    def _L0_ffn_setup():
        import jax, jax.numpy as jnp
        import numpy as np
        B, S, D, DFF = (4, 1024, 512, 2048)
        CAPACITY_FACTOR = 0.5
        K = int(CAPACITY_FACTOR * S)
        key = jax.random.key(seed)
        ks = jax.random.split(key, 5)
        hidden_states = jax.random.normal(ks[0], (B, S, D), dtype=jnp.float32)
        router_weight = jax.random.normal(ks[1], (D,), dtype=jnp.float32) * 0.02
        router_bias = jnp.zeros((1,), dtype=jnp.float32)
        w1 = jax.random.normal(ks[2], (D, DFF), dtype=jnp.float32) * (1.0 / np.sqrt(D))
        b1 = jnp.zeros((DFF,), dtype=jnp.float32)
        w2 = jax.random.normal(ks[3], (DFF, D), dtype=jnp.float32) * (1.0 / np.sqrt(DFF))
        b2 = jnp.zeros((D,), dtype=jnp.float32)
        return {'hidden_states': hidden_states, 'router_weight': router_weight, 'router_bias': router_bias, 'w1': w1, 'b1': b1, 'w2': w2, 'b2': b2}
    _L0_ffn_all = _L0_ffn_setup()
    _L0_ffn_in = {k: v for k, v in _L0_ffn_all.items() if k in ('router_weight', 'router_bias', 'w1', 'b1', 'w2', 'b2')}
    del _L0_ffn_all

    def _L1_xattn_setup():
        import jax, jax.numpy as jnp
        import numpy as np
        DIM = 512
        CTX_DIM = 256
        N_HEADS = 32
        HEAD_DIM = DIM // N_HEADS
        POS_DIM = 2
        B, N, CTXN = (2, 512, 512)
        ROPE_BASE = 10000.0

        def apply_axial_rope(x, pos):
            b, n, h, d = x.shape
            p = pos.shape[-1]
            dpa = d // p
            half = dpa // 2
            freqs = ROPE_BASE ** (-jnp.arange(half, dtype=x.dtype) / half)
            ang = pos[..., :, None] * freqs
            cos = jnp.cos(ang)[:, :, None, :, :]
            sin = jnp.sin(ang)[:, :, None, :, :]
            xr = x.reshape(b, n, h, p, half, 2)
            x1, x2 = (xr[..., 0], xr[..., 1])
            out = jnp.stack([x1 * cos - x2 * sin, x1 * sin + x2 * cos], axis=-1)
            return out.reshape(b, n, h, d)
        key = jax.random.key(seed)
        ks = jax.random.split(key, 8)
        x = jax.random.normal(ks[0], (B, N, DIM), jnp.float32)
        ctx = jax.random.normal(ks[1], (B, CTXN, CTX_DIM), jnp.float32)
        pos_map = jax.random.uniform(ks[2], (B, N, POS_DIM), jnp.float32)
        ctx_pos_map = jax.random.uniform(ks[3], (B, CTXN, POS_DIM), jnp.float32)
        Wq = jax.random.normal(ks[4], (DIM, DIM), jnp.float32) / np.sqrt(DIM)
        Wkv = jax.random.normal(ks[5], (CTX_DIM, 2 * DIM), jnp.float32) / np.sqrt(CTX_DIM)
        Wout = jax.random.normal(ks[6], (DIM, DIM), jnp.float32) / np.sqrt(DIM)
        bout = jnp.zeros((DIM,), jnp.float32)
        return {'x': x, 'ctx': ctx, 'pos_map': pos_map, 'ctx_pos_map': ctx_pos_map, 'Wq': Wq, 'Wkv': Wkv, 'Wout': Wout, 'bout': bout}
    _L1_xattn_all = _L1_xattn_setup()
    _L1_xattn_in = {k: v for k, v in _L1_xattn_all.items() if k in ('Wq', 'Wkv', 'Wout', 'bout')}
    del _L1_xattn_all

    def _L1_ffn_setup():
        import jax, jax.numpy as jnp
        import numpy as np
        B, S, D_IN, D_OUT = (4, 512, 512, 512)
        EPS = 1e-10
        key = jax.random.key(seed)
        kx, kw, kb = jax.random.split(key, 3)
        x = jax.random.normal(kx, (B, S, D_IN), dtype=jnp.float32)
        weight = jax.random.normal(kw, (D_OUT, D_IN), dtype=jnp.float32) * 0.02
        bias = jax.random.normal(kb, (D_OUT,), dtype=jnp.float32) * 0.02
        return {'x': x, 'weight': weight, 'bias': bias}
    _L1_ffn_all = _L1_ffn_setup()
    _L1_ffn_in = {k: v for k, v in _L1_ffn_all.items() if k in ('weight', 'bias')}
    del _L1_ffn_all
    return {'x': x, 'ctx_1024': ctx_1024, 'fside_BxSx2_0': fside_BxSx2_0, 'L0_xattn_Wq': _L0_xattn_in['Wq'], 'L0_xattn_bq': _L0_xattn_in['bq'], 'L0_xattn_Wk': _L0_xattn_in['Wk'], 'L0_xattn_bk': _L0_xattn_in['bk'], 'L0_ffn_router_weight': _L0_ffn_in['router_weight'], 'L0_ffn_router_bias': _L0_ffn_in['router_bias'], 'L0_ffn_w1': _L0_ffn_in['w1'], 'L0_ffn_b1': _L0_ffn_in['b1'], 'L0_ffn_w2': _L0_ffn_in['w2'], 'L0_ffn_b2': _L0_ffn_in['b2'], 'L1_xattn_Wq': _L1_xattn_in['Wq'], 'L1_xattn_Wkv': _L1_xattn_in['Wkv'], 'L1_xattn_Wout': _L1_xattn_in['Wout'], 'L1_xattn_bout': _L1_xattn_in['bout'], 'L1_ffn_weight': _L1_ffn_in['weight'], 'L1_ffn_bias': _L1_ffn_in['bias']}

def reference(x, ctx_1024, fside_BxSx2_0, L0_xattn_Wq, L0_xattn_bq, L0_xattn_Wk, L0_xattn_bk, L0_ffn_router_weight, L0_ffn_router_bias, L0_ffn_w1, L0_ffn_b1, L0_ffn_w2, L0_ffn_b2, L1_xattn_Wq, L1_xattn_Wkv, L1_xattn_Wout, L1_xattn_bout, L1_ffn_weight, L1_ffn_bias):
    import jax
    import jax.numpy as jnp

    def _L0_xattn_ref(teacher_logits, teacher_features, Wq, bq, Wk, bk):
        import jax, jax.numpy as jnp
        import numpy as np
        query = jnp.einsum('bnc,dc->bnd', teacher_features, Wq) + bq
        key = jnp.einsum('bnc,dc->bnd', teacher_features, Wk) + bk
        energy = jnp.einsum('bnd,bmd->bnm', query, key)
        attention = jax.nn.softmax(energy, axis=-1)
        x_m = jnp.einsum('bln,bmn->blm', teacher_logits, attention)
        return x_m

    def _L0_ffn_ref(hidden_states, router_weight, router_bias, w1, b1, w2, b2):
        import jax, jax.numpy as jnp
        import numpy as np
        B, S, D, DFF = (4, 1024, 512, 2048)
        CAPACITY_FACTOR = 0.5
        K = int(CAPACITY_FACTOR * S)
        b, s, d = hidden_states.shape
        scores = jnp.einsum('bsd,d->bs', hidden_states, router_weight) + router_bias[0]
        top_scores, indices = jax.lax.top_k(scores, K)
        weights = jax.nn.sigmoid(top_scores)
        selected = jnp.take_along_axis(hidden_states, indices[:, :, None], axis=1)
        h = jax.nn.gelu(jnp.einsum('bkd,df->bkf', selected, w1) + b1)
        processed = jnp.einsum('bkf,fd->bkd', h, w2) + b2
        weighted = processed * weights[:, :, None]
        flat = hidden_states.reshape(b * s, d)
        flat_idx = (indices + jnp.arange(b)[:, None] * s).reshape(-1)
        out = flat.at[flat_idx].add(weighted.reshape(b * K, d))
        return out.reshape(b, s, d)

    def _L1_xattn_ref(x, ctx, pos_map, ctx_pos_map, Wq, Wkv, Wout, bout):
        import jax, jax.numpy as jnp
        import numpy as np
        DIM = 512
        CTX_DIM = 256
        N_HEADS = 32
        HEAD_DIM = DIM // N_HEADS
        POS_DIM = 2
        B, N, CTXN = (2, 512, 512)
        ROPE_BASE = 10000.0

        def apply_axial_rope(x, pos):
            b, n, h, d = x.shape
            p = pos.shape[-1]
            dpa = d // p
            half = dpa // 2
            freqs = ROPE_BASE ** (-jnp.arange(half, dtype=x.dtype) / half)
            ang = pos[..., :, None] * freqs
            cos = jnp.cos(ang)[:, :, None, :, :]
            sin = jnp.sin(ang)[:, :, None, :, :]
            xr = x.reshape(b, n, h, p, half, 2)
            x1, x2 = (xr[..., 0], xr[..., 1])
            out = jnp.stack([x1 * cos - x2 * sin, x1 * sin + x2 * cos], axis=-1)
            return out.reshape(b, n, h, d)
        b, n, _ = x.shape
        ctx_n = ctx.shape[1]
        q = (x @ Wq).reshape(b, n, N_HEADS, HEAD_DIM)
        k, v = jnp.split(ctx @ Wkv, 2, axis=-1)
        k = k.reshape(b, ctx_n, N_HEADS, HEAD_DIM)
        v = v.reshape(b, ctx_n, N_HEADS, HEAD_DIM)
        q = apply_axial_rope(q, pos_map)
        k = apply_axial_rope(k, ctx_pos_map)
        scale = 1.0 / np.sqrt(HEAD_DIM).astype(np.float32)
        logits = jnp.einsum('bqhd,bkhd->bhqk', q, k) * scale
        w = jax.nn.softmax(logits, axis=-1)
        attn = jnp.einsum('bhqk,bkhd->bqhd', w, v)
        attn = attn.reshape(b, n, N_HEADS * HEAD_DIM)
        return attn @ Wout + bout

    def _L1_ffn_ref(x, weight, bias):
        import jax, jax.numpy as jnp
        import numpy as np
        B, S, D_IN, D_OUT = (4, 512, 512, 512)
        EPS = 1e-10
        scale = jnp.mean(jnp.abs(weight))
        w_t = jnp.clip(jnp.round(weight / (scale + EPS)), -1.0, 1.0)
        w_ste = weight + jax.lax.stop_gradient(w_t * scale - weight)
        return jnp.einsum('bsi,oi->bso', x, w_ste) + bias
    x = x + _L0_xattn_ref(_layernorm(x, axis=-1), ctx_1024, L0_xattn_Wq, L0_xattn_bq, L0_xattn_Wk, L0_xattn_bk)
    x = x + _L0_ffn_ref(_layernorm(x, axis=-1), L0_ffn_router_weight, L0_ffn_router_bias, L0_ffn_w1, L0_ffn_b1, L0_ffn_w2, L0_ffn_b2)
    x = x + _L1_xattn_ref(_layernorm(x, axis=-1), ctx_1024, fside_BxSx2_0, fside_BxSx2_0, L1_xattn_Wq, L1_xattn_Wkv, L1_xattn_Wout, L1_xattn_bout)
    x = x + _L1_ffn_ref(_layernorm(x, axis=-1), L1_ffn_weight, L1_ffn_bias)
    return x

_drawn_inputs = setup_inputs


def setup_inputs(seed=0):
    import zlib

    import numpy as np

    out = dict(_drawn_inputs(seed))
    spreads = {'L0_xattn_bq': (0.0, 0.1),
     'L0_xattn_bk': (0.0, 0.8),
     'L0_ffn_b1': (0.0, 0.547),
     'L0_ffn_b2': (0.0, 0.38),
     'L1_xattn_bout': (0.0, 0.1)}
    factors = {'fside_BxSx2_0': 4.19, 'L1_ffn_bias': 6.75}
    for name, (base, spread) in spreads.items():
        noise = np.random.default_rng([zlib.crc32(name.encode()), seed]).standard_normal(out[name].shape)
        drawn = base * np.exp(spread * noise) if base else spread * noise
        out[name] = jnp.asarray(drawn.astype(out[name].dtype))
    for name, factor in factors.items():
        out[name] = (out[name] * factor).astype(out[name].dtype)
    return out
```

```python
from contextlib import ExitStack

import concourse.bass as bass
import concourse.mybir as mybir
import numpy as np

F32 = mybir.dt.float32
F32R = mybir.dt.float32r
ACT = mybir.ActivationFunctionType
ALU = mybir.AluOpType
AX = mybir.AxisListType

P = 128
B, S, D = 4, 512, 512
C = 256
DQK = 128
DFF = 2048
H, HD = 32, 16
NT = S // P
KF = D // P
KC = C // P
FB = DFF // 512
W = 512
LN_EPS = 1e-5
TERNARY_EPS = 1e-10
ROPE_BASE = 10000.0
HALF = 4

QUADS = H // 4
PAIRS = 2
ROW_MAX = 48
RING = 4

A_GROUPS = 18
A_HI = 14


def attention_schedule():
    order = []
    for step in range(-3, QUADS + 1):
        for slot in range(8):
            if slot == 2 and 0 <= step + 1 < QUADS:
                order.append(("R", step + 1, 0))
            if 0 <= step < QUADS:
                order.append(("QK", step, slot))
            if 0 <= step + 2 < QUADS:
                order += [("M", step + 2, 2 * slot), ("M", step + 2, 2 * slot + 1)]
            if slot % 2 == 1 and 0 <= step + 3 < QUADS:
                order.append(("S", step + 3, slot // 2))
            if slot == 1 and 0 <= step - 1 < QUADS:
                order.append(("AV", step - 1, NT - 1))
            if slot in (3, 5, 7) and 0 <= step < QUADS:
                order.append(("AV", step, slot // 2 - 1))
            if slot == 6 and 0 <= step - 1 < QUADS:
                order.append(("O", step - 1, 0))
    return order


SCHEDULE = attention_schedule()
C_LNT, C_Q, C_K, C_V, C_ATT = 0, 4, 8, 12, 16
ATT_GROUP = {}
for _e in SCHEDULE:
    if _e[0] in ("M", "R", "O"):
        ATT_GROUP[_e] = C_ATT + len(ATT_GROUP)
C_AT = C_ATT + len(ATT_GROUP)
C_OUT, C_LNT2, C_FF = C_AT + 4, C_AT + 8, C_AT + 12
C_GROUPS = C_AT + 16
C_HI = 12
assert C_GROUPS % 2 == 0


def build(nc, t):
    with ExitStack() as ctx:
        def sb(name, shape, dt=F32, stack=ctx):
            return stack.enter_context(nc.sbuf_tensor(name, shape, dt))

        def sem(name):
            return ctx.enter_context(nc.semaphore(name))

        banks = ctx.enter_context(nc.psum_tensor("banks", [P, 8, W], F32))
        bank = [banks[:, i, :] for i in range(8)]

        x = sb("x", [P, B * NT, D])
        ident = sb("ident_sb", [P, P])
        b1 = sb("b1_sb", [P, DFF // P])
        rb = sb("rb_sb", [P, 1])
        minus_rb = sb("minus_rb", [P, 1])
        router = sb("router", [P, B * NT])
        cosd = sb("cosd", [P, B * NT, 2 * HALF, 2])
        sind = sb("sind", [P, B * NT, 2 * HALF, 2])
        mv = sb("mv", [P, NT, 2])
        stats = sb("stats", [P, NT, 6])
        rstd = sb("rstd", [P, NT])
        minus_half = sb("minus_half", [P, NT])
        small = sb("small", [P, 4 * NT])

        ab = ExitStack()
        x2h = sb("x2h", [P, B, KF, S], F32R, ab)
        x2l = sb("x2l", [P, B, KF, S], F32R, ab)
        ph_a = ExitStack()
        xn = sb("xn", [P, NT, D], F32, ph_a)
        xth = sb("xth", [P, KF, S], F32R, ph_a)
        xtl = sb("xtl", [P, KF, S], F32R, ph_a)
        ct = sb("ct", [P, KC, S], F32, ph_a)
        cth = sb("cth", [P, KC, S], F32R, ph_a)
        ctl = sb("ctl", [P, KC, S], F32R, ph_a)
        qh, ql, kh, kl = (sb(n, [P, S], F32R, ph_a) for n in ("qh", "ql", "kh", "kl"))
        att = sb("att", [P, NT, S], F32, ph_a)
        atth = sb("atth", [P, NT, S], F32R, ph_a)
        attl = sb("attl", [P, NT, S], F32R, ph_a)
        wqk = sb("wqk", [P, 2, KC, DQK], F32, ph_a)
        wqkh = sb("wqkh", [P, 2, KC, DQK], F32R, ph_a)
        wqkl = sb("wqkl", [P, 2, KC, DQK], F32R, ph_a)
        bqk = sb("bqk", [P, 2], F32, ph_a)
        rw = sb("rw_sb", [P, D], F32, ph_a)
        b2 = sb("b2_sb", [P, D], F32, ph_a)
        pos = sb("pos_sb", [P, B * NT, 2], F32, ph_a)
        ang = sb("ang", [P, 2, B * NT, 2, HALF], F32, ph_a)
        turns = sb("turns", [P, 2 * B * NT * 2 * HALF], F32, ph_a)
        nmax = sb("nmax", [P, NT], F32, ph_a)
        rsum = sb("rsum", [P, NT], F32, ph_a)
        scratch = sb("scratch", [P, D], F32, ph_a)
        ph_a.close()

        ph_b = ExitStack()
        w1h, w1l, w2h, w2l = (sb(n, [P, 2, KF, 512], F32R, ph_b) for n in ("w1h", "w1l", "w2h", "w2l"))
        wst = sb("wst", [P, 4, 2, 512], F32, ph_b)
        g = sb("g", [P, 4, S], F32, ph_b)
        gh = sb("gh", [P, 4, S], F32R, ph_b)
        gl = sb("gl", [P, 4, S], F32R, ph_b)
        ph_b.close()
        ab.close()

        wqh = sb("wqh", [P, KF, D], F32R)
        wql = sb("wql", [P, KF, D], F32R)
        wkvh = sb("wkvh", [P, KC, 2 * D], F32R)
        wkvl = sb("wkvl", [P, KC, 2 * D], F32R)
        woh = sb("woh", [P, KF, D], F32R)
        wol = sb("wol", [P, KF, D], F32R)
        tern = sb("tern", [P, KF, D], F32R)
        boutb = sb("bout_sb", [P, D])
        biasb = sb("bias_sb", [P, D])
        tok = sb("tok", [P, NT, D])
        ph_c0 = ExitStack()
        yth = sb("yth", [P, KF, S], F32R, ph_c0)
        ytl = sb("ytl", [P, KF, S], F32R, ph_c0)
        ph_c0.close()
        wt = sb("wt", [P, 4, 2, S])
        qr = sb("qr", [P, NT, H, HD])
        kr = sb("kr", [P, NT, H, HD])
        va = sb("va", [P, NT, H, HD + 1])
        stg = sb("stg", [P, 2, 2, NT, 4, 64])
        nmx = sb("nmx", [P, 2, NT, 4])
        nms = sb("nms", [P, NT, 4, 2])
        mrow = sb("mrow", [8, 2, S])
        ots = sb("ots", [P, 2, S])
        rinv = sb("rinv", [P, 2, NT, 4])
        scl = sb("scl", [P, 4])
        ph_c1 = ExitStack()
        dt_ = sb("dt_", [P, KC, S], F32, ph_c1)
        dth = sb("dth", [P, KC, S], F32R, ph_c1)
        dtl = sb("dtl", [P, KC, S], F32R, ph_c1)
        ra = sb("ra", [P, 2, D], F32, ph_c1)
        rbuf = sb("rbuf", [P, 2, D], F32, ph_c1)
        ph_c1.close()
        qst = sb("qst", [P, RING, PAIRS, S], F32R)
        kst = sb("kst", [P, RING, PAIRS, S], F32R)

        ld_const, ld_x, ld_ct = sem("ld_const"), sem("ld_x"), sem("ld_ct")
        tab, tab_sin = sem("tab"), sem("tab_sin")
        wqk_hi, wqk_lo = sem("wqk_hi"), sem("wqk_lo")
        ln_stats, ln_agg, ln_eps, ln_rstd, ln_xn = (sem("ln_" + n) for n in ("stats", "agg", "eps", "rstd", "xn"))
        ct_hi, ct_lo = sem("ct_hi"), sem("ct_lo")
        a_ready, a_free, a_hi = sem("a_ready"), sem("a_free"), sem("a_hi")
        e_ready, e_max, e_exp, e_rec, e_att = (sem("e_" + n) for n in ("ready", "max", "exp", "rec", "att"))
        rt_z, rt_exp, rt_den, rt_w, x_res, x_b2 = (sem(n) for n in ("rt_z", "rt_exp", "rt_den", "rt_w", "x_res", "x_b2"))
        w_ld = sem("w_ld")
        w_hi, w_lo = sem("w_hi"), sem("w_lo")
        f1_ready, f1_gelu, g_hi, g_lo, f2_ready, f2_free = (sem(n) for n in ("f1_ready", "f1_gelu", "g_hi", "g_lo", "f2_ready", "f2_free"))
        cw_ld, cw_hi, cw_lo = sem("cw_ld"), sem("cw_hi"), sem("cw_lo")
        tn_sum, tn_all, tn_scale, tn_done = (sem("tn_" + n) for n in ("sum", "all", "scale", "done"))
        ld_cb = sem("ld_cb")
        dt_ld, dt_hi, dt_lo = sem("dt_ld"), sem("dt_hi"), sem("dt_lo")
        v_ready, v_free, c_hi = sem("v_ready"), sem("v_free"), sem("c_hi")
        rope_mul, rope_done = sem("rope_mul"), sem("rope_done")
        ones_set, stg_hi, stg_done = sem("ones_set"), sem("stg_hi"), sem("stg_done")
        s_ready, s_done, lt_ready, exp_done, av_done, ot_done = (
            sem(n) for n in ("s_ready", "s_done", "lt_ready", "exp_done", "av_done", "ot_done"))
        nm_hi, nm_lo, mx_dma, o_rinv = sem("nm_hi"), sem("nm_lo"), sem("mx_dma"), sem("o_rinv")
        ot_init = sem("ot_init")
        x_bias, st_out = sem("x_bias"), sem("st_out")

        block = ctx.enter_context(nc.Block())

        def f32(ap):
            return ap.bitcast(F32)

        def r32(ap):
            return ap.bitcast(F32R)

        def wait_apart(eng, sem_, value):
            value = eng.to_reg(value)
            eng.wait_ge(ld_const, 16 * N_CONST)
            eng.wait_ge(sem_, value)

        def three(ah, al, bh, bl):
            return ((ah, bh), (ah, bl), (al, bh))

        STARTED = (ct_lo, a_free, e_exp, f1_gelu, f2_free, v_free, exp_done, s_done, ot_done,
                   a_ready, g_lo, g_hi, lt_ready, av_done, v_ready, x_res, ln_xn, rope_done, s_ready)

        N_CONST = 10
        C_WEIGHTS = ("l1_wq", "l1_wkv", "l1_wout", "l1_wt")

        @block.sync
        def _(sp):
            for counted in STARTED:
                sp.sem_inc(counted, 1)
            for dst, name in ((ident, "ident"), (b1, "b1"), (rb, "rb"), (bqk, "bqk"), (rw, "rw"), (b2, "b2"),
                              (pos, "pos")):
                sp.dma_start(dst[:], t[name]).then_inc(ld_const, 16)
            for j, name in enumerate(("l0_wq", "l0_wk")):
                sp.dma_start(wqk[:, j], t[name].rearrange("(k p) d -> p k d", p=P)).then_inc(ld_const, 16)
            sp.dma_start(minus_half[:], t["minus_half"]).then_inc(ld_const, 16)
            with sp.Fori(0, B) as b:
                sp.dma_start(x[:, bass.ds(b * NT, NT), :], t["x"][b].rearrange("(i p) d -> p i d", p=P)).then_inc(ld_x, 16)
                sp.wait_ge(ct_lo, 1 + b)
                sp.dma_start(ct[:], t["ctx"][b].rearrange("(k p) n -> p k n", p=P)).then_inc(ld_ct, 16)
                wait_apart(sp, ld_x, 16 * (b + 1))

            sp.wait_ge(x_b2, NT * B)
            sp.wait_ge(a_ready, 1 + A_GROUPS * B)
            for n in range(FB * 4):
                fb, c = divmod(n, 4)
                if n >= 4:
                    sp.wait_ge(w_hi, 2 * (n - 3))
                    sp.wait_ge(w_lo, 2 * (n - 3))
                sp.dma_start(wst[:, c, 0], t["w1"][c * P:(c + 1) * P, fb * 512:(fb + 1) * 512]).then_inc(w_ld, 16)
                sp.dma_start(wst[:, c, 1], t["w2"][(4 * fb + c) * P:(4 * fb + c + 1) * P, :]).then_inc(w_ld, 16)
                sp.wait_ge(w_ld, 32 * (n + 1))

            sp.wait_ge(f2_free, 1 + 4 * B * FB)
            sp.dma_start(boutb[:], t["bout"]).then_inc(ld_cb, 16)
            sp.dma_start(biasb[:], t["bias"]).then_inc(ld_cb, 16)
            for n, name in enumerate(C_WEIGHTS):
                stage = (qr, kr)[n % 2]
                if n >= 2:
                    sp.wait_ge(cw_hi, n - 1)
                    sp.wait_ge(cw_lo, n - 1)
                cols = 1024 if name == "l1_wkv" else 512
                sp.dma_start(stage[:].rearrange("p i h d -> p (i h d)").rearrange("p (k n) -> p k n", n=cols),
                             t[name].rearrange("(k p) n -> p k n", p=P)).then_inc(cw_ld, 16)
                sp.wait_ge(cw_ld, 16 * (n + 1))
            with sp.Fori(0, B) as b:
                sp.wait_ge(av_done, 1 + 32 * b)
                sp.dma_start(dt_[:], t["ctx"][b].rearrange("(k p) n -> p k n", p=P)).then_inc(dt_ld, 16)
                for u in range(QUADS):
                    sp.wait_ge(v_free, 1 + C_GROUPS * b + ATT_GROUP["R", u, 0] + 1)
                    for pr in range(PAIRS):
                        for hp in range(2):
                            row = 4 * pr + 2 * hp
                            sp.dma_start(f32(qst[64 * hp + ROW_MAX:64 * hp + ROW_MAX + 2, u % RING, pr, :]),
                                         mrow[row:row + 2, u % 2, :]).then_inc(mx_dma, 16)
                sp.wait_ge(v_free, 1 + C_GROUPS * (b + 1))
                sp.dma_start(t["out"][b].rearrange("(i p) d -> p i d", p=P), x[:, bass.ds(b * NT, NT), :]).then_inc(st_out, 16)
            sp.wait_ge(st_out, 16 * B)

        @block.tensor
        def _(pe):
            def transposes(dst_bank, src, rows=P):
                for i in range(NT):
                    last = pe.transpose(dst_bank[0:rows, i * P:(i + 1) * P], src(i), ident[:])
                return last

            def product(dst, terms):
                for n, (a_, b_) in enumerate(terms):
                    last = pe.matmul(dst, a_, b_, start=(n == 0), stop=(n == len(terms) - 1))
                return last

            pe.wait_ge(ld_const, 16 * N_CONST)
            pe.wait_ge(wqk_lo, 1)
            pe.wait_ge(wqk_hi, 1)
            with pe.Fori(0, B) as b:
                def a_bank(n):
                    pe.wait_ge(a_free, 1 + A_GROUPS * b + max(0, n - 3))
                    return bank[n % 4]

                for k in range(KF):
                    dst = a_bank(k)
                    if k == 0:
                        pe.wait_ge(ln_xn, 1 + 2 * NT * b + NT)
                    transposes(dst, lambda i: xn[:, i, k * P:(k + 1) * P]).then_inc(a_ready, 1)
                pe.wait_ge(ct_hi, b + 1)
                pe.wait_ge(ct_lo, 1 + b + 1)
                for j in range(2):
                    product(a_bank(4 + j)[:], [m for k in range(KC) for m in three(
                        wqkh[:, j, k, :], wqkl[:, j, k, :], cth[:, k, :], ctl[:, k, :])]).then_inc(a_ready, 1)
                pe.wait_ge(a_free, 1 + A_GROUPS * b + 6)
                for i in range(NT):
                    rows = slice(i * P, (i + 1) * P)
                    pe.wait_ge(e_exp, 1 + NT * b)
                    product(bank[4 + i][:], three(qh[:, rows], ql[:, rows], kh[:], kl[:])).then_inc(e_ready, 1)
                pe.wait_ge(e_att, NT * (b + 1))
                for k in range(NT):
                    transposes(a_bank(6 + k), lambda i: att[:, i, k * P:(k + 1) * P]).then_inc(a_ready, 1)
                pe.wait_ge(a_free, 1 + A_GROUPS * b + 10)
                for i in range(NT):
                    rows = slice(i * P, (i + 1) * P)
                    product(a_bank(10 + i)[:], [m for k in range(NT) for m in three(
                        xth[:, k, rows], xtl[:, k, rows], atth[:, k, :], attl[:, k, :])]).then_inc(a_ready, 1)
                pe.wait_ge(ln_xn, 1 + 2 * NT * b + 2 * NT)
                for k in range(KF):
                    transposes(a_bank(14 + k), lambda i: xn[:, i, k * P:(k + 1) * P]).then_inc(a_ready, 1)

            pe.wait_ge(a_free, 1 + A_GROUPS * B)
            pe.wait_ge(e_exp, 1 + NT * B)
            for fb in range(FB):
                par = fb % 2
                pe.wait_ge(w_hi, 8 * (fb + 1))
                pe.wait_ge(w_lo, 8 * (fb + 1))
                with pe.Fori(0, B) as b:
                    it = b + fb * B
                    for f in range(4):
                        pe.wait_ge(f1_gelu, 1 + 4 * it)
                        cols = slice(f * P, (f + 1) * P)
                        product(bank[f][:], [m for k in range(KF) for m in three(
                            w1h[:, par, k, cols], w1l[:, par, k, cols],
                            x2h[:, bass.ds(b, 1), k, :].rearrange("p o n -> p (o n)"),
                            x2l[:, bass.ds(b, 1), k, :].rearrange("p o n -> p (o n)"))]).then_inc(f1_ready, 1)
                    pe.wait_ge(f2_free, 1 + 4 * it)
                    for f in range(4):
                        pe.wait_ge(g_hi, 1 + 4 * it + f + 1)
                        pe.wait_ge(g_lo, 1 + 4 * it + f + 1)
                        for i in range(NT):
                            rows = slice(i * P, (i + 1) * P)
                            terms = three(gh[:, f, rows], gl[:, f, rows], w2h[:, par, f, :], w2l[:, par, f, :])
                            for n, (a_, b_) in enumerate(terms):
                                last = pe.matmul(bank[4 + i][:], a_, b_, start=(f == 0 and n == 0),
                                                 stop=(f == 3 and n == 2))
                            if f == 3:
                                last.then_inc(f2_ready, 1)

            pe.wait_ge(f2_free, 1 + 4 * B * FB)
            pe.wait_ge(tn_sum, 1)
            pe.wait_ge(ones_set, 1)
            pe.matmul(bank[6][:, 0:2], stg[:, 0, 0].rearrange("p i h r -> p (i h r)")[:, 0:P], scl[:, 0:2],
                      start=True, stop=True).then_inc(tn_all, 1)
            pe.wait_ge(tn_scale, 1)
            pe.wait_ge(cw_lo, 3)
            pe.wait_ge(cw_hi, 4)
            pe.wait_ge(ot_init, 1)
            with pe.Fori(0, B) as b:
                def v_bank(n):
                    pe.wait_ge(v_free, 1 + C_GROUPS * b + max(0, n - 1))
                    return bank[6 + n % 2]

                pe.wait_ge(ln_xn, 1 + 2 * NT * B + 2 * NT * b + NT)
                for k in range(KF):
                    transposes(v_bank(C_LNT + k), lambda i: tok[:, i, k * P:(k + 1) * P]).then_inc(v_ready, 1)
                pe.wait_ge(v_free, 1 + C_GROUPS * b + C_LNT + 4)
                for i in range(NT):
                    rows = slice(i * P, (i + 1) * P)
                    product(v_bank(C_Q + i)[:], [m for k in range(KF) for m in three(
                        yth[:, k, rows], ytl[:, k, rows], wqh[:, k, :], wql[:, k, :])]).then_inc(v_ready, 1)
                pe.wait_ge(dt_hi, b + 1)
                pe.wait_ge(dt_lo, b + 1)
                for c0, half in ((C_K, 0), (C_V, 1)):
                    for i in range(NT):
                        rows = slice(i * P, (i + 1) * P)
                        cols = slice(half * D, (half + 1) * D)
                        product(v_bank(c0 + i)[:], [m for k in range(KC) for m in three(
                            dth[:, k, rows], dtl[:, k, rows], wkvh[:, k, cols], wkvl[:, k, cols])]).then_inc(v_ready, 1)

                for ev in SCHEDULE:
                    kind, u, n = ev
                    ring = u % RING
                    if kind == "S":
                        pr, what = divmod(n, 2)
                        if n == 0:
                            pe.wait_ge(stg_done, QUADS * b + u + 1)
                        pe.wait_ge(s_done, 1 + 4 * QUADS * b + 4 * u + n)
                        transposes(bank[5], lambda i: stg[:, u % 2, what, i, 2 * pr:2 * pr + 2, :].rearrange(
                            "p h r -> p (h r)")).then_inc(s_ready, 1)
                    elif kind == "M":
                        i, h = divmod(n, 4)
                        if n == 0:
                            pe.wait_ge(s_done, 1 + 4 * QUADS * b + 4 * (u + 1))
                        r = 64 * (h % 2)
                        pe.matmul(v_bank(ATT_GROUP[ev])[:], qst[r:r + 64, ring, h // 2, i * P:(i + 1) * P],
                                  kst[r:r + 64, ring, h // 2, :], start=True, stop=True).then_inc(v_ready, 1)
                    elif kind == "R":
                        pe.wait_ge(nm_lo, QUADS * b + u + 1)
                        transposes(v_bank(ATT_GROUP[ev]), lambda i: nms[:, i].rearrange("p h s -> p (h s)"),
                                   rows=8).then_inc(v_ready, 1)
                    elif kind == "QK":
                        kt, pr = divmod(n, 2)
                        gi = 8 * u + n
                        if n == 0:
                            pe.wait_ge(mx_dma, 64 * (QUADS * b + u + 1))
                        pe.wait_ge(exp_done, 1 + 8 * QUADS * b + max(0, gi - 1))
                        for hp in range(2):
                            r = 64 * hp
                            last = pe.matmul(bank[2 * (gi % 2) + hp][:], kst[r:r + 64, ring, pr, kt * P:(kt + 1) * P],
                                             qst[r:r + 64, ring, pr, :], start=True, stop=True)
                        last.then_inc(lt_ready, 1)
                    elif kind == "AV":
                        if n == 0:
                            pe.wait_ge(ot_done, 1 + QUADS * b + u)
                        pe.wait_ge(exp_done, 1 + 8 * QUADS * b + 8 * u + 2 * n + 2)
                        for h in range(4):
                            gi = 8 * u + 2 * n + h // 2
                            last = pe.matmul(bank[4][32 * h:32 * h + HD + 1, :], va[:, n, 4 * u + h, :],
                                             wt[:, gi % 4, h % 2, :], start=(n == 0), stop=(n == NT - 1))
                        last.then_inc(av_done, 1)
                    else:
                        pe.wait_ge(ot_done, 1 + QUADS * b + u + 1)
                        transposes(v_bank(ATT_GROUP[ev]), lambda i: ots[:, u % 2, i * P:(i + 1) * P]).then_inc(v_ready, 1)

                pe.wait_ge(v_free, 1 + C_GROUPS * b + C_AT)
                for k in range(KF):
                    transposes(v_bank(C_AT + k), lambda i: tok[:, i, k * P:(k + 1) * P]).then_inc(v_ready, 1)
                pe.wait_ge(v_free, 1 + C_GROUPS * b + C_AT + 4)
                for i in range(NT):
                    rows = slice(i * P, (i + 1) * P)
                    product(v_bank(C_OUT + i)[:], [m for k in range(KF) for m in three(
                        yth[:, k, rows], ytl[:, k, rows], woh[:, k, :], wol[:, k, :])]).then_inc(v_ready, 1)
                pe.wait_ge(ln_xn, 1 + 2 * NT * B + 2 * NT * (b + 1))
                for k in range(KF):
                    transposes(v_bank(C_LNT2 + k), lambda i: tok[:, i, k * P:(k + 1) * P]).then_inc(v_ready, 1)
                pe.wait_ge(v_free, 1 + C_GROUPS * b + C_LNT2 + 4)
                for i in range(NT):
                    rows = slice(i * P, (i + 1) * P)
                    product(v_bank(C_FF + i)[:], [m for k in range(KF) for m in (
                        (yth[:, k, rows], tern[:, k, :]), (ytl[:, k, rows], tern[:, k, :]))]).then_inc(v_ready, 1)

        @block.scalar
        def _(act):
            act.wait_ge(tab, 8)
            for n, dst in ((0, cosd), (1, sind)):
                a_ = ang[:, n].rearrange("p t a f -> p t (a f)")
                act.activation(dst[:, :, :, 0], a_, ACT.Sin, scale=1.0 if n == 0 else -1.0).then_inc(tab_sin, 1)
                act.activation(dst[:, :, :, 1], a_, ACT.Sin).then_inc(tab_sin, 1)
            act.wait_ge(ld_const, 16 * N_CONST)
            act.activation(wqkh[:], wqk[:], ACT.Copy).then_inc(wqk_hi, 1)
            with act.Fori(0, B) as b:
                def hi(n, n_hi, dst):
                    act.wait_ge(a_ready, 1 + A_GROUPS * b + n + 1)
                    act.activation(dst, bank[n % 4][:], ACT.Copy).then_inc(a_hi, 1)

                act.wait_ge(ld_ct, 16 * (b + 1))
                act.wait_ge(a_ready, 1 + A_GROUPS * b)
                act.activation(cth[:], ct[:], ACT.Copy).then_inc(ct_hi, 1)
                for k in range(KF):
                    hi(k, k, xth[:, k, :])
                for j, dst in enumerate((qh, kh)):
                    act.wait_ge(a_ready, 1 + A_GROUPS * b + 5 + j)
                    act.activation(dst[:], bank[j][:], ACT.Identity, bias=bqk[:, j:j + 1]).then_inc(a_hi, 1)
                for i in range(NT):
                    act.wait_ge(e_max, NT * b + i + 1)
                    act.activation(att[:, i, :], bank[4 + i][:], ACT.Exp, bias=nmax[:, i:i + 1],
                                   accum_out=rsum[:, i:i + 1]).then_inc(e_exp, 1)
                for k in range(NT):
                    hi(6 + k, 6 + k, atth[:, k, :])
                for k in range(KF):
                    hi(14 + k, 10 + k, x2h[:, bass.ds(b, 1), k, :].rearrange("p o n -> p (o n)"))
                act.wait_ge(rt_z, NT * (b + 1))
                act.activation(small[:, NT:2 * NT], small[:, 0:NT], ACT.Exp, scale=-1.0,
                               bias=minus_rb[:, 0:1]).then_inc(rt_exp, 1)

            act.wait_ge(a_free, 1 + A_GROUPS * B)
            act.wait_ge(x_b2, NT * B)
            for fb in range(FB):
                with act.Fori(0, B) as b:
                    it = b + fb * B
                    act.wait_ge(g_lo, 1 + 4 * it)
                    act.wait_ge(g_hi, 1 + 4 * it)
                    for f in range(4):
                        act.wait_ge(f1_ready, 4 * it + f + 1)
                        act.activation(g[:, f, :], bank[f][:], ACT.Gelu_apprx_tanh,
                                       bias=b1[:, 4 * fb + f:4 * fb + f + 1]).then_inc(f1_gelu, 1)

            act.wait_ge(f2_free, 1 + 4 * B * FB)
            act.wait_ge(tn_scale, 1)
            with act.Fori(0, B) as b:
                def hi_c(n, dst):
                    act.wait_ge(v_ready, 1 + C_GROUPS * b + n + 1)
                    act.activation(dst, bank[6 + n % 2][:], ACT.Copy).then_inc(c_hi, 1)

                act.wait_ge(dt_ld, 16 * (b + 1))
                act.activation(dth[:], dt_[:], ACT.Copy).then_inc(dt_hi, 1)
                for k in range(KF):
                    hi_c(C_LNT + k, yth[:, k, :])
                for kind, u, n in SCHEDULE:
                    if kind == "S":
                        pr, what = divmod(n, 2)
                        act.wait_ge(lt_ready, 1 + 8 * QUADS * b + 8 * max(0, u - RING + 1))
                        act.wait_ge(s_ready, 1 + 4 * QUADS * b + 4 * u + n + 1)
                        act.activation((qst, kst)[what][:, u % RING, pr, :], bank[5][:], ACT.Copy).then_inc(s_done, 1)
                    elif kind == "QK":
                        gi = 8 * u + n
                        act.wait_ge(lt_ready, 1 + 8 * QUADS * b + gi + 1)
                        act.wait_ge(av_done, 1 + 4 * QUADS * b + max(0, (gi - 4) // 2 + 1))
                        two = 2 * (gi % 2)
                        act.activation(wt[:, gi % 4, :, :], banks[:, two:two + 2, :], ACT.Exp,
                                       scale=float(HD) ** -0.5).then_inc(exp_done, 1)
                    elif kind == "AV" and n == NT - 1:
                        act.wait_ge(av_done, 1 + 4 * QUADS * b + 4 * u + 4)
                        act.wait_ge(v_ready, 1 + C_GROUPS * b + (ATT_GROUP["O", u - 2, 0] + 1 if u >= 2 else 0))
                        act.activation(ots[:, u % 2, :], bank[4][:], ACT.Copy).then_inc(ot_done, 1)
                for k in range(KF):
                    hi_c(C_AT + k, yth[:, k, :])
                for k in range(KF):
                    hi_c(C_LNT2 + k, yth[:, k, :])

        @block.vector
        def _(dve):
            def layer_norm(n, x_tile, dst):
                for i in range(NT):
                    dve.bn_stats(stats[:, i, :], x_tile(i)).then_inc(ln_stats, 1)
                for i in range(NT):
                    wait_apart(dve, ln_stats, NT * n + i + 1)
                    dve.bn_aggr(mv[:, i, :], stats[:, i, :]).then_inc(ln_agg, 1)
                dve.wait_ge(ln_rstd, n + 1)
                for i in range(NT):
                    dve.tensor_scalar(dst[:, i, :], x_tile(i), mv[:, i, 0:1], rstd[:, i:i + 1],
                                      ALU.subtract, ALU.mult).then_inc(ln_xn, 1)

            two_pi = 2 * np.pi
            c1 = 6.28125
            c2 = float(np.round((two_pi - c1) * 2.0 ** 20)) / 2.0 ** 20
            c3 = two_pi - c1 - c2
            magic = 1.5 * 2.0 ** 23
            dve.wait_ge(ld_const, 16 * N_CONST)
            dve.tensor_scalar(minus_rb[:], rb[:], -1.0, None, ALU.mult)
            freqs = (np.float32(ROPE_BASE) ** (-np.arange(HALF, dtype=np.float32) / np.float32(HALF))).astype(np.float32)
            for f in range(HALF):
                last = dve.tensor_scalar(ang[:, 1, :, :, f], pos[:], float(freqs[f]), None, ALU.mult)
            last.then_inc(tab, 1)
            dve.wait_ge(tab, 1)
            dve.tensor_scalar(ang[:, 0], ang[:, 1], float(np.pi / 2), None, ALU.add).then_inc(tab, 1)
            dve.wait_ge(tab, 2)
            both = ang[:, 0:2].rearrange("p n t a f -> p (n t a f)")
            dve.tensor_scalar(turns[:], both, 1.0 / two_pi, magic, ALU.mult, ALU.add).then_inc(tab, 1)
            dve.wait_ge(tab, 3)
            dve.tensor_scalar(turns[:], turns[:], magic, None, ALU.subtract).then_inc(tab, 1)
            for n, c in enumerate((c1, c2, c3)):
                dve.wait_ge(tab, 4 + n)
                dve.scalar_tensor_tensor(both, turns[:], -c, both, ALU.mult, ALU.add).then_inc(tab, 1)
            dve.wait_ge(tab, 7)
            dve.tensor_scalar(both, both, 3.1415925, -3.1415925, ALU.min, ALU.max).then_inc(tab, 1)

            with dve.Fori(0, B) as b:
                def x_tile(i):
                    return x[:, bass.ds(NT * b + i, 1), :].rearrange("p o n -> p (o n)")

                def lo(n, n_hi, dst, dst_hi, bias=None):
                    dve.wait_ge(a_hi, A_HI * b + n_hi + 1)
                    if bias is None:
                        last = dve.tensor_tensor(dst, bank[n % 4][:], f32(dst_hi), ALU.subtract)
                    else:
                        last = dve.scalar_tensor_tensor(dst, bank[n % 4][:], bias, f32(dst_hi), ALU.add, ALU.subtract)
                    last.then_inc(a_free, 1)

                wait_apart(dve, ld_x, 16 * (b + 1))
                dve.wait_ge(a_ready, 1 + A_GROUPS * b)
                dve.wait_ge(x_res, 1 + NT * b)
                layer_norm(2 * b, x_tile, xn)
                for k in range(KF):
                    lo(k, k, xtl[:, k, :], xth[:, k, :])
                for j, (dst, dst_hi) in enumerate(((ql, qh), (kl, kh))):
                    lo(4 + j, 4 + j, dst[:], dst_hi[:], bqk[:, j:j + 1])
                for i in range(NT):
                    dve.wait_ge(e_ready, NT * b + i + 1)
                    dve.tensor_reduce(nmax[:, i:i + 1], bank[4 + i][:], AX.X, ALU.max, negate=True).then_inc(e_max, 1)
                for i in range(NT):
                    dve.wait_ge(e_exp, 1 + NT * b + i + 1)
                    dve.reciprocal(small[:, 12 + i:13 + i], rsum[:, i:i + 1]).then_inc(e_rec, 1)
                    dve.wait_ge(e_rec, NT * b + i + 1)
                    dve.tensor_scalar(att[:, i, :], att[:, i, :], small[:, 12 + i:13 + i], None, ALU.mult).then_inc(e_att, 1)
                for k in range(NT):
                    lo(6 + k, 6 + k, attl[:, k, :], atth[:, k, :])
                for i in range(NT):
                    dve.wait_ge(a_ready, 1 + A_GROUPS * b + 11 + i)
                    dve.tensor_tensor(x_tile(i), bank[(10 + i) % 4][:], x_tile(i), ALU.add).then_inc(a_free, 1)
                wait_apart(dve, a_free, 1 + A_GROUPS * b + 14)
                layer_norm(2 * b + 1, x_tile, xn)
                dve.wait_ge(ln_xn, 1 + NT * (2 * b + 2))
                for i in range(NT):
                    if i:
                        dve.wait_ge(rt_z, NT * b + i)
                    dve.tensor_tensor_reduce(scratch[:], xn[:, i, :], rw[:], 1.0, 0.0, ALU.mult, ALU.add,
                                             small[:, i:i + 1]).then_inc(rt_z, 1)
                for k in range(KF):
                    lo(14 + k, 10 + k, x2l[:, bass.ds(b, 1), k, :].rearrange("p o n -> p (o n)"),
                       x2h[:, bass.ds(b, 1), k, :].rearrange("p o n -> p (o n)"))
                dve.wait_ge(rt_exp, b + 1)
                dve.tensor_scalar(small[:, 2 * NT:3 * NT], small[:, NT:2 * NT], 1.0, None, ALU.add).then_inc(rt_den, 1)
                dve.wait_ge(rt_den, b + 1)
                dve.reciprocal(router[:, bass.ds(NT * b, NT)], small[:, 2 * NT:3 * NT]).then_inc(rt_w, 1)
                dve.wait_ge(rt_w, b + 1)
                for i in range(NT):
                    dve.wait_ge(x_res, 1 + NT * b + i + 1)
                    dve.scalar_tensor_tensor(x_tile(i), b2[:], router[:, bass.ds(NT * b + i, 1)], x_tile(i),
                                             ALU.mult, ALU.add).then_inc(x_b2, 1)

            dve.wait_ge(x_b2, NT * B)
            dve.wait_ge(a_ready, 1 + A_GROUPS * B)

            def split_hi(fb, c):
                dve.wait_ge(w_ld, 32 * (4 * fb + c + 1))
                for j, dst in enumerate((w1h, w2h)):
                    dve.tensor_copy(dst[:, fb % 2, bass.ds(c, 1), :], wst[:, bass.ds(c, 1), j, :]).then_inc(w_hi, 1)

            for c in range(4):
                split_hi(0, c)
            for fb in range(FB):
                with dve.Fori(0, B) as b:
                    it = b + fb * B
                    for f in range(4):
                        dve.wait_ge(f1_gelu, 1 + 4 * it + f + 1)
                        dve.tensor_copy(gh[:, f, :], g[:, f, :]).then_inc(g_hi, 1)
                    if fb + 1 < FB:
                        dve.wait_ge(f2_ready, 4 * B * fb)
                        split_hi(fb + 1, b)
                    for i in range(NT):
                        x_i = x[:, bass.ds(NT * b + i, 1), :].rearrange("p o n -> p (o n)")
                        dve.wait_ge(f2_ready, 4 * it + i + 1)
                        dve.scalar_tensor_tensor(x_i, bank[4 + i][:], router[:, bass.ds(NT * b + i, 1)], x_i,
                                                 ALU.mult, ALU.add).then_inc(f2_free, 1)

            dve.wait_ge(f2_free, 1 + 4 * B * FB)
            dve.memset(bank[4][:], 0.0).then_inc(ot_init, 1)
            dve.memset(va[:].rearrange("p i h d -> p (i h d)"), 1.0)

            def stage(n):
                return (qr, kr)[n % 2][:].rearrange("p i h d -> p (i h d)")

            for n, dst in enumerate((wqh, wkvh, woh)):
                dve.wait_ge(cw_ld, 16 * (n + 1))
                dve.tensor_copy(dst[:].rearrange("p k n -> p (k n)"), stage(n)).then_inc(cw_hi, 1)
            dve.wait_ge(cw_ld, 64)
            wlin = stage(3)
            dve.memset(scl[:, 1:2], 0.0)
            dve.tensor_reduce(scl[:, 0:1], wlin, AX.X, ALU.add, apply_absolute_value=True).then_inc(tn_sum, 1)
            dve.wait_ge(tn_all, 1)
            dve.tensor_scalar(scl[:, 2:3], bank[6][:, 0:1], 1.0 / (D * D), TERNARY_EPS, ALU.mult, ALU.add)
            dve.tensor_scalar(scl[:, 3:4], bank[6][:, 0:1], -1.0 / (D * D), None, ALU.mult).then_inc(tn_scale, 1)
            dve.wait_ge(tn_scale, 1)
            dve.tensor_scalar(scl[:, 0:1], scl[:, 2:3], 0.5, None, ALU.mult)
            dve.tensor_scalar(scl[:, 1:2], scl[:, 2:3], -0.5, None, ALU.mult).then_inc(tn_done, 1)
            dve.wait_ge(tn_done, 1)
            above = stage(4)
            dve.wait_ge(cw_lo, 3)
            dve.tensor_scalar(above, wlin, scl[:, 0:1], None, ALU.is_gt).then_inc(tn_done, 1)
            dve.wait_ge(tn_done, 2)
            dve.scalar_tensor_tensor(tern[:].rearrange("p k n -> p (k n)"), wlin, scl[:, 1:2], above,
                                     ALU.is_lt, ALU.subtract).then_inc(cw_hi, 1)
            dve.wait_ge(cw_hi, 4)

            with dve.Fori(0, B) as b:
                def x_tile(i):
                    return x[:, bass.ds(NT * b + i, 1), :].rearrange("p o n -> p (o n)")

                def lo_c(n, n_hi, dst, dst_hi):
                    dve.wait_ge(c_hi, C_HI * b + n_hi + 1)
                    dve.tensor_tensor(dst, bank[6 + n % 2][:], f32(dst_hi), ALU.subtract).then_inc(v_free, 1)

                def ready(n):
                    dve.wait_ge(v_ready, 1 + C_GROUPS * b + n + 1)
                    return bank[6 + n % 2]

                wait_apart(dve, v_ready, 1 + C_GROUPS * b)
                layer_norm(2 * B + 2 * b, x_tile, tok)
                for k in range(KF):
                    lo_c(C_LNT + k, k, ytl[:, k, :], yth[:, k, :])
                for c0, slot0 in ((C_Q, 0), (C_K, NT)):
                    for i in range(NT):
                        z = ready(c0 + i)
                        n = slot0 + i
                        if n >= 2:
                            dve.wait_ge(rope_done, 1 + 2 * NT * b + n - 1)
                        else:
                            dve.wait_ge(rope_done, 1 + 2 * NT * b)
                        cos_i, sin_i = (tb[:, bass.ds(NT * b + i, 1), :, :] for tb in (cosd, sind))
                        zh = z[:].rearrange("p (h f) -> p h f", h=H)
                        dve.tensor_tensor(ra[:, n % 2, :].rearrange("p (h f) -> p h f", h=H), zh,
                                          cos_i.rearrange("p o f e -> p o (f e)").to_broadcast([P, H, HD]), ALU.mult)
                        z2 = z[:].rearrange("p (h f e) -> p h f e", h=H, e=2)
                        r2 = rbuf[:, n % 2, :].rearrange("p (h f e) -> p h f e", h=H, e=2)
                        for e in range(2):
                            last = dve.tensor_tensor(r2[:, :, :, e], z2[:, :, :, 1 - e],
                                                     sin_i[:, :, :, e].to_broadcast([P, H, 2 * HALF]), ALU.mult)
                        last.then_inc(v_free, 1)
                for i in range(NT):
                    dve.tensor_copy(va[:, i, :, 0:HD], ready(C_V + i)[:].rearrange("p (h d) -> p h d", h=H)).then_inc(v_free, 1)
                for ev in SCHEDULE:
                    kind, u, n = ev
                    if kind == "M":
                        i, h = divmod(n, 4)
                        dve.tensor_reduce(nmx[:, u % 2, i, h:h + 1], ready(ATT_GROUP[ev])[:], AX.X, ALU.max,
                                          negate=True).then_inc(v_free, 1)
                        if n == 15:
                            dve.wait_ge(v_free, 1 + C_GROUPS * b + ATT_GROUP[ev] + 1)
                            dve.tensor_copy(r32(nms[:, :, :, 0]), nmx[:, u % 2]).then_inc(nm_hi, 1)
                            dve.wait_ge(nm_hi, QUADS * b + u + 1)
                            dve.tensor_tensor(nms[:, :, :, 1], nmx[:, u % 2], nms[:, :, :, 0], ALU.subtract).then_inc(nm_lo, 1)
                    elif kind == "R":
                        dve.tensor_copy(mrow[:, u % 2, :], ready(ATT_GROUP[ev])[0:8, :]).then_inc(v_free, 1)
                    elif kind == "O":
                        o = ready(ATT_GROUP[ev])[:].rearrange("p (i h r) -> p i h r", i=NT, h=4)
                        dve.reciprocal(rinv[:, u % 2], o[:, :, :, HD]).then_inc(o_rinv, 1)
                        dve.wait_ge(o_rinv, QUADS * b + u + 1)
                        dve.tensor_tensor(tok[:, :, 64 * u:64 * u + 64].rearrange("p i (h d) -> p i h d", h=4),
                                          o[:, :, :, 0:HD], rinv[:, u % 2].unsqueeze(3).to_broadcast([P, NT, 4, HD]),
                                          ALU.mult).then_inc(v_free, 1)
                for k in range(KF):
                    lo_c(C_AT + k, 4 + k, ytl[:, k, :], yth[:, k, :])
                dve.wait_ge(x_bias, 2 * NT * b + NT)
                for i in range(NT):
                    dve.tensor_tensor(x_tile(i), ready(C_OUT + i)[:], x_tile(i), ALU.add).then_inc(v_free, 1)
                wait_apart(dve, v_free, 1 + C_GROUPS * b + C_OUT + NT)
                layer_norm(2 * B + 2 * b + 1, x_tile, tok)
                for k in range(KF):
                    lo_c(C_LNT2 + k, 8 + k, ytl[:, k, :], yth[:, k, :])
                dve.wait_ge(x_bias, 2 * NT * b + 2 * NT)
                for i in range(NT):
                    z = ready(C_FF + i)
                    dve.scalar_tensor_tensor(x_tile(i), z[:], scl[:, 3:4], x_tile(i), ALU.mult, ALU.add).then_inc(v_free, 1)

        @block.gpsimd
        def _(pool):
            def rstd_of(n):
                wait_apart(pool, ln_agg, NT * (n + 1))
                wait_apart(pool, ln_xn, 1 + NT * n)
                pool.tensor_scalar(rstd[:], mv[:, :, 1], LN_EPS, 1.0, ALU.add, ALU.mult).then_inc(ln_eps, 1)
                pool.wait_ge(ln_eps, n + 1)
                pool.tensor_tensor(rstd[:], rstd[:], minus_half[:], ALU.pow).then_inc(ln_rstd, 1)

            pool.wait_ge(ld_const, 16 * N_CONST)
            pool.wait_ge(wqk_hi, 1)
            pool.tensor_tensor(wqkl[:], wqk[:], f32(wqkh[:]), ALU.subtract).then_inc(wqk_lo, 1)
            with pool.Fori(0, B) as b:
                pool.wait_ge(ct_hi, b + 1)
                pool.tensor_tensor(ctl[:], ct[:], f32(cth[:]), ALU.subtract).then_inc(ct_lo, 1)
                rstd_of(2 * b)
                rstd_of(2 * b + 1)
                for i in range(NT):
                    x_i = x[:, bass.ds(NT * b + i, 1), :].rearrange("p o n -> p (o n)")
                    wait_apart(pool, ln_xn, 1 + NT * (2 * b + 1) + i + 1)
                    pool.tensor_tensor(x_i, x_i, xn[:, i, :], ALU.add).then_inc(x_res, 1)

            pool.wait_ge(a_ready, 1 + A_GROUPS * B)

            def split_lo(fb, c):
                wait_apart(pool, w_hi, 2 * (4 * fb + c + 1))
                for j, (dst, hi_) in enumerate(((w1l, w1h), (w2l, w2h))):
                    pool.tensor_tensor(dst[:, fb % 2, bass.ds(c, 1), :], wst[:, bass.ds(c, 1), j, :],
                                       f32(hi_[:, fb % 2, bass.ds(c, 1), :]), ALU.subtract).then_inc(w_lo, 1)

            for c in range(4):
                split_lo(0, c)
            for fb in range(FB):
                with pool.Fori(0, B) as b:
                    it = b + fb * B
                    for f in range(4):
                        pool.wait_ge(g_hi, 1 + 4 * it + f + 1)
                        pool.tensor_tensor(gl[:, f, :], g[:, f, :], f32(gh[:, f, :]), ALU.subtract).then_inc(g_lo, 1)
                    if fb + 1 < FB:
                        split_lo(fb + 1, b)

            pool.wait_ge(f2_free, 1 + 4 * B * FB)
            pool.memset(stg[:].rearrange("p q w i h r -> p (q w i h r)"), 1.0).then_inc(ones_set, 1)
            for n, (dst, hi_) in enumerate(((wql, wqh), (wkvl, wkvh), (wol, woh))):
                pool.wait_ge(cw_hi, n + 1)
                pool.tensor_tensor(dst[:].rearrange("p k n -> p (k n)"),
                                   (qr, kr)[n % 2][:].rearrange("p i h d -> p (i h d)"),
                                   f32(hi_[:].rearrange("p k n -> p (k n)")), ALU.subtract).then_inc(cw_lo, 1)
            pool.wait_ge(tn_all, 1)
            for par in range(2):
                pool.memset(stg[:, par, 0, :, :, ROW_MAX:64], 0.0)
                last = pool.memset(stg[:, par, 1, :, :, ROW_MAX + 2:64], 0.0)
            pool.wait_ge(cw_hi, 4)
            pool.wait_ge(ld_cb, 32)
            with pool.Fori(0, B) as b:
                rstd_of(2 * B + 2 * b)
                pool.wait_ge(dt_hi, b + 1)
                pool.tensor_tensor(dtl[:], dt_[:], f32(dth[:]), ALU.subtract).then_inc(dt_lo, 1)

                def add_bias(n, bias):
                    for i in range(NT):
                        x_i = x[:, bass.ds(NT * b + i, 1), :].rearrange("p o n -> p (o n)")
                        wait_apart(pool, ln_xn, 1 + NT * (2 * B + 2 * b + n) + i + 1)
                        pool.tensor_tensor(x_i, x_i, bias[:], ALU.add).then_inc(x_bias, 1)

                add_bias(0, boutb)
                for c0, dst in ((C_Q, qr), (C_K, kr)):
                    for i in range(NT):
                        n = c0 - C_Q + i
                        pool.wait_ge(v_free, 1 + C_GROUPS * b + c0 + i + 1)
                        pool.tensor_tensor(dst[:, i].rearrange("p h d -> p (h d)"), ra[:, n % 2, :], rbuf[:, n % 2, :],
                                           ALU.add).then_inc(rope_done, 1)
                for u in range(QUADS):
                    heads = slice(4 * u, 4 * u + 4)
                    if u == 0:
                        wait_apart(pool, rope_done, 1 + 2 * NT * (b + 1))
                    wait_apart(pool, s_ready, 1 + 4 * QUADS * b + 4 * max(0, u - 1))
                    for what, src, lo_at, hi_at in ((0, qr, 1, 2), (1, kr, 2, 1)):
                        sv = stg[:, u % 2, what].rearrange("p i h (j d) -> p i h j d", j=4)
                        src_u = src[:, :, heads, :]
                        pool.tensor_copy(r32(sv[:, :, :, 0, :]), src_u)
                        pool.tensor_copy(r32(sv[:, :, :, hi_at, :]), src_u).then_inc(stg_hi, 1)
                        pool.wait_ge(stg_hi, 2 * QUADS * b + 2 * u + what + 1)
                        last = pool.tensor_tensor(sv[:, :, :, lo_at, :], src_u, sv[:, :, :, 0, :], ALU.subtract)
                    last.then_inc(stg_done, 1)
                rstd_of(2 * B + 2 * b + 1)
                add_bias(1, biasb)


def layouts(np_, v):
    c = np_.ascontiguousarray

    def over(a):
        return c(np_.broadcast_to(a.reshape(1, -1), (P, a.size)))

    return {
        "x": c(v["x"]),
        "ctx": c(v["ctx_1024"].transpose(0, 2, 1)),
        "pos": c(v["fside_BxSx2_0"].reshape(B * NT, P, 2).transpose(1, 0, 2)),
        "l0_wq": c(v["L0_xattn_Wq"].T),
        "l0_wk": c(v["L0_xattn_Wk"].T),
        "bqk": c(np_.stack([v["L0_xattn_bq"], v["L0_xattn_bk"]], axis=1)),
        "rw": over(v["L0_ffn_router_weight"]),
        "rb": over(v["L0_ffn_router_bias"]),
        "w1": c(v["L0_ffn_w1"]),
        "b1": c(v["L0_ffn_b1"].reshape(DFF // P, P).T),
        "w2": c(v["L0_ffn_w2"]),
        "b2": over(v["L0_ffn_b2"]),
        "l1_wq": c(v["L1_xattn_Wq"]),
        "l1_wkv": c(v["L1_xattn_Wkv"]),
        "l1_wout": c(v["L1_xattn_Wout"]),
        "bout": over(v["L1_xattn_bout"]),
        "l1_wt": c(v["L1_ffn_weight"].T),
        "bias": over(v["L1_ffn_bias"]),
        "ident": np_.eye(P, dtype=np_.float32),
        "minus_half": np_.full((P, NT), -0.5, np_.float32),
    }


def kernel(**inputs):
    import concourse.bacc as bacc
    from concourse.bass_utils import run_bass_kernel_spmd

    arrays = layouts(np, {k: np.asarray(v) for k, v in inputs.items()})
    nc = bacc.Bacc("TRN2", target_bir_lowering=False, num_devices=1)
    t = {k: nc.dram_tensor("in_" + k, a.shape, mybir.dt.from_np(a.dtype), kind="ExternalInput").ap() for k, a in arrays.items()}
    t["out"] = nc.dram_tensor("out", (B, S, D), F32, kind="ExternalOutput").ap()
    build(nc, t)
    arrays = {"in_" + k: a for k, a in arrays.items()}
    return run_bass_kernel_spmd(nc, [arrays], core_ids=[0]).results[0]["out"]
```

```python
from contextlib import ExitStack

import concourse.bass as bass
import concourse.mybir as mybir
import numpy as np

F32 = mybir.dt.float32
F32R = mybir.dt.float32r
ACT = mybir.ActivationFunctionType
ALU = mybir.AluOpType
AX = mybir.AxisListType

P = 128
B, S, D = 4, 512, 512
C = 256
DQK = 128
DFF = 2048
H, HD = 32, 16
NT = S // P
KF = D // P
KC = C // P
FB = DFF // 512
W = 512
LN_EPS = 1e-5
TERNARY_EPS = 1e-10
ROPE_BASE = 10000.0
HALF = 4

QUADS = H // 4
PAIRS = 2
ROW_MAX = 48
RING = 4
NQ = B * QUADS

A_PER = 18
A_RING = 3
E_BANK = 4


def attention_step(s):
    order = []
    for slot in range(8):
        order.append(("M", s + 2, 2 * slot))
        if slot % 2 == 0:
            order.append(("S", s + 3, slot // 2))
        if slot == 1:
            order.append(("AV", s - 1, NT - 1))
        if slot in (3, 5, 7):
            order.append(("AV", s, slot // 2 - 1))
        order.append(("M", s + 2, 2 * slot + 1))
        order.append(("QK", s, slot))
        if slot == 2:
            order.append(("R", s + 1, 0))
        if slot == 4:
            order.append(("O", s - 1, 0))
    return [e for e in order if 0 <= e[1] < NQ]


V_NUMBER = {}
for _s in range(-3, NQ + 1):
    for _e in attention_step(_s):
        if _e[0] in ("M", "R", "O"):
            V_NUMBER[_e] = len(V_NUMBER)
C2_HEAD = range(-3, 1)
C2_BODY = 4
C2_LOOPS = (NQ - 4) // C2_BODY
C2_TAIL = range(1 + C2_BODY * C2_LOOPS, NQ + 1)
V_PER = 18 * C2_BODY



def build(nc, t):
    with ExitStack() as ctx:
        def sb(name, shape, dt=F32, stack=ctx):
            return stack.enter_context(nc.sbuf_tensor(name, shape, dt))

        def sem(name):
            return ctx.enter_context(nc.semaphore(name))

        banks = ctx.enter_context(nc.psum_tensor("banks", [P, 8, W], F32))
        bank = [banks[:, i, :] for i in range(8)]

        x = sb("x", [P, B * NT, D])
        ident = sb("ident_sb", [P, P])
        b1 = sb("b1_sb", [P, DFF // P])
        rb = sb("rb_sb", [P, 1])
        minus_rb = sb("minus_rb", [P, 1])
        router = sb("router", [P, B * NT])
        mv = sb("mv", [P, NT, 2])
        stats = sb("stats", [P, NT, 6])
        rstd = sb("rstd", [P, NT])
        minus_half = sb("minus_half", [P, NT])
        small = sb("small", [P, 4 * NT])
        scl = sb("scl", [P, 4])
        cosd = sb("cosd", [P, B * NT, 2 * HALF, 2])
        sind = sb("sind", [P, B * NT, 2 * HALF, 2])
        ones = cosd[:].rearrange("p t f e -> p (t f e)")[:, 0:P]

        ab = ExitStack()
        x2h = sb("x2h", [P, B, KF, S], F32R, ab)
        x2l = sb("x2l", [P, B, KF, S], F32R, ab)
        ph_a = ExitStack()
        xn1 = sb("xn1", [P, NT, D], F32, ph_a)
        xn2 = sb("xn2", [P, NT, D], F32, ph_a)
        xth = sb("xth", [P, KF, S], F32R, ph_a)
        xtl = sb("xtl", [P, KF, S], F32R, ph_a)
        ct = sb("ct", [P, KC, S], F32, ph_a)
        cth = sb("cth", [P, KC, S], F32R, ph_a)
        ctl = sb("ctl", [P, KC, S], F32R, ph_a)
        qh, ql, kh, kl = (sb(n, [P, S], F32R, ph_a) for n in ("qh", "ql", "kh", "kl"))
        att = sb("att", [P, NT, S], F32, ph_a)
        atth = sb("atth", [P, NT, S], F32R, ph_a)
        attl = sb("attl", [P, NT, S], F32R, ph_a)
        wqk = sb("wqk", [P, 2, KC, DQK], F32, ph_a)
        wqkh = sb("wqkh", [P, 2, KC, DQK], F32R, ph_a)
        wqkl = sb("wqkl", [P, 2, KC, DQK], F32R, ph_a)
        bqk = sb("bqk", [P, 2], F32, ph_a)
        rw = sb("rw_sb", [P, D], F32, ph_a)
        b2 = sb("b2_sb", [P, D], F32, ph_a)
        pos = sb("pos_sb", [P, B * NT, 2], F32, ph_a)
        ang = sb("ang", [P, 2, B * NT, 2, HALF], F32, ph_a)
        turns = sb("turns", [P, 2 * B * NT * 2 * HALF], F32, ph_a)
        nmax = sb("nmax", [P, NT], F32, ph_a)
        rsum = sb("rsum", [P, NT], F32, ph_a)
        scratch = sb("scratch", [P, D], F32, ph_a)
        ph_a.close()

        ph_b = ExitStack()
        even = [sb(n, [P, KF, 512], F32R, ph_b) for n in ("w1h0", "w1l0", "w2h0", "w2l0")]
        odd = [sb(n, [P, KF, 512], F32R, ph_b) for n in ("w1h1", "w1l1", "w2h1", "w2l1")]
        w1h, w1l, w2h, w2l = zip(even, odd)
        wst = sb("wst", [P, 4, 2, 512], F32, ph_b)
        g = sb("g", [P, 4, S], F32, ph_b)
        gh = sb("gh", [P, 4, S], F32R, ph_b)
        gl = sb("gl", [P, 4, S], F32R, ph_b)
        ph_b.close()
        ab.close()

        qr = sb("qr", [P, NQ, NT, 64])
        kr_stack = ExitStack()
        kr = sb("kr", [P, NQ, NT, 64], F32, kr_stack)
        even_place = ExitStack()
        sb("even_place", [P, 4, KF, 512], F32, even_place)
        vr_stack = ExitStack()
        vr = sb("vr", [P, NQ, NT, 64], F32, vr_stack)
        wqh, wql = even[0], even[1]
        wkvh, wkvl = (w[:].rearrange("p k n -> p (k n)").rearrange("p (k n) -> p k n", k=KC) for w in even[2:])
        ph_c1 = ExitStack()
        tok = sb("tok", [P, NT, D], F32, ph_c1)
        yth = sb("yth", [P, KF, S], F32R, ph_c1)
        ytl = sb("ytl", [P, KF, S], F32R, ph_c1)
        dt_ = sb("dt_", [P, KC, S], F32, ph_c1)
        dth = sb("dth", [P, KC, S], F32R, ph_c1)
        dtl = sb("dtl", [P, KC, S], F32R, ph_c1)
        rbuf = sb("rbuf", [P, 2, D], F32, ph_c1)
        ph_c1.close()

        ph_c2 = ExitStack()
        qst = sb("qst", [P, RING, PAIRS, S], F32R, ph_c2)
        kst = sb("kst", [P, RING, PAIRS, S], F32R, ph_c2)
        nmx = sb("nmx", [P, 2, NT, 4], F32, ph_c2)
        nms = sb("nms", [P, NT, 4, 2], F32, ph_c2)
        mrow = sb("mrow", [8, 2, S], F32, ph_c2)
        ots = sb("ots", [P, S], F32, ph_c2)
        rinv = sb("rinv", [P, 2, NT, 4], F32, ph_c2)
        va = sb("va", [P, 2, NT, 4, HD + 1], F32, ph_c2)
        ph_c2.close()
        vr_stack.close()
        even_place.close()
        ph_c2 = ExitStack()
        stg = sb("stg", [P, 2, 2, NT, 4, 64], F32, ph_c2)
        wt = sb("wt", [P, 4, 2, S], F32, ph_c2)
        ph_c2.close()
        kr_stack.close()

        woh = sb("woh", [P, KF, D], F32R)
        wol = sb("wol", [P, KF, D], F32R)
        tern = sb("tern", [P, KF, D], F32R)
        wraw = sb("wraw", [P, KF, D])
        boutb = sb("bout_sb", [P, D])
        biasb = sb("bias_sb", [P, D])
        atok = sb("atok", [P, NT, D])
        ath = sb("ath", [P, KF, S], F32R)
        atl = sb("atl", [P, KF, S], F32R)
        ftok = sb("ftok", [P, NT, D])
        fth = sb("fth", [P, KF, S], F32R)
        ftl = sb("ftl", [P, KF, S], F32R)

        ld_const, ld_x, ld_ct = sem("ld_const"), sem("ld_x"), sem("ld_ct")
        tab, tab_sin = sem("tab"), sem("tab_sin")
        wqk_hi, wqk_lo = sem("wqk_hi"), sem("wqk_lo")
        ln_stats, ln_agg, ln_eps, ln_rstd, ln_xn = (sem("ln_" + n) for n in ("stats", "agg", "eps", "rstd", "xn"))
        ct_hi, ct_lo = sem("ct_hi"), sem("ct_lo")
        a_ready, a_free, a_hi = sem("a_ready"), sem("a_free"), sem("a_hi")
        e_ready, e_max, e_exp, e_rec, e_att = (sem("e_" + n) for n in ("ready", "max", "exp", "rec", "att"))
        rt_z, rt_exp, rt_den, rt_w, x_res, x_b2 = (sem(n) for n in ("rt_z", "rt_exp", "rt_den", "rt_w", "x_res", "x_b2"))
        w_ld, w_hi, w_lo = sem("w_ld"), sem("w_hi"), sem("w_lo")
        f1_ready, f1_gelu, g_hi, g_lo, f2_ready, f2_free = (sem(n) for n in ("f1_ready", "f1_gelu", "g_hi", "g_lo", "f2_ready", "f2_free"))
        q_ready, q_free, q_hi = sem("q_ready"), sem("q_free"), sem("q_hi")
        dt_ld, dt_hi, dt_lo = sem("dt_ld"), sem("dt_hi"), sem("dt_lo")
        v_copied = sem("v_copied")
        rope_done = sem("rope_done")
        ones_set, stg_zero, stg_hi, stg_done = sem("ones_set"), sem("stg_zero"), sem("stg_hi"), sem("stg_done")
        va_done = sem("va_done")
        v_ready, v_free = sem("v_ready"), sem("v_free")
        s_ready, s_done, lt_ready, exp_done, av_done, ot_done = (
            sem(n) for n in ("s_ready", "s_done", "lt_ready", "exp_done", "av_done", "ot_done"))
        nm_hi, nm_lo, mx_dma, o_rinv = sem("nm_hi"), sem("nm_lo"), sem("mx_dma"), sem("o_rinv")
        ot_init = sem("ot_init")
        cw_ld, cw_hi, cw_lo, ld_cb = sem("cw_ld"), sem("cw_hi"), sem("cw_lo"), sem("ld_cb")
        tn_sum, tn_all, tn_scale, tn_done = (sem("tn_" + n) for n in ("sum", "all", "scale", "done"))
        at_copy, o_ready, o_free, o_hi = sem("at_copy"), sem("o_ready"), sem("o_free"), sem("o_hi")
        bo_done = sem("bo_done")
        x_bias, st_out = sem("x_bias"), sem("st_out")

        block = ctx.enter_context(nc.Block())

        def f32(ap):
            return ap.bitcast(F32)

        def r32(ap):
            return ap.bitcast(F32R)

        STARTED = tuple((s, 1) for s in (f1_gelu, f2_free, g_lo, g_hi, q_ready, rope_done, dt_lo, ln_xn)) + (
            (q_free, 4), (v_copied, 4))

        N_CONST = 10

        def wait_apart(eng, sem_, value):
            value = eng.to_reg(value)
            eng.wait_ge(ld_const, 16 * N_CONST)
            eng.wait_ge(sem_, value)

        def three(ah, al, bh, bl):
            return ((ah, bh), (ah, bl), (al, bh))

        A_HEAD = 10
        HI_HEAD, HI_PER = 10, 14

        def a_first(j):
            return A_HEAD + A_PER * j

        def hi_first(j):
            return HI_HEAD + HI_PER * j

        def a_slot(n0, n):
            return (n if isinstance(n0, int) and n0 == 0 else A_HEAD + n) % A_RING

        def o_first(b):
            return 16 * b - 8

        def tile_of(b, i):
            return x[:, bass.ds(NT * b + i, 1), :].rearrange("p o n -> p (o n)")

        @block.sync
        def _(sp):
            for counted, start in STARTED:
                sp.sem_inc(counted, start)
            for j, name in enumerate(("l0_wq", "l0_wk")):
                sp.dma_start(wqk[:, j], t[name].rearrange("(k p) d -> p k d", p=P)).then_inc(ld_const, 16)
            for dst, name in ((bqk, "bqk"), (ident, "ident"), (minus_half, "minus_half"), (b1, "b1"), (rb, "rb"),
                              (rw, "rw"), (b2, "b2"), (pos, "pos")):
                sp.dma_start(dst[:], t[name]).then_inc(ld_const, 16)
            for b in range(B):
                if b:
                    sp.wait_ge(ct_lo, b)
                sp.dma_start(ct[:], t["ctx"][b].rearrange("(k p) n -> p k n", p=P)).then_inc(ld_ct, 16)
                sp.dma_start(x[:, NT * b:NT * (b + 1), :], t["x"][b].rearrange("(i p) d -> p i d", p=P)).then_inc(ld_x, 16)
                sp.wait_ge(ld_x, 16 * (b + 1))

            sp.wait_ge(x_b2, NT * B)
            sp.wait_ge(a_ready, a_first(B - 1) + 8)

            def wait_slot(n):
                if n >= 4:
                    sp.wait_ge(w_hi, 2 * (n - 3))
                    sp.wait_ge(w_lo, 2 * (n - 3))

            for n in range(FB * 4):
                fb, c = divmod(n, 4)
                wait_slot(n)
                sp.dma_start(wst[:, c, 0], t["w1"][c * P:(c + 1) * P, fb * 512:(fb + 1) * 512]).then_inc(w_ld, 16)
                sp.dma_start(wst[:, c, 1], t["w2"][(4 * fb + c) * P:(4 * fb + c + 1) * P, :]).then_inc(w_ld, 16)
                sp.wait_ge(w_ld, 32 * (n + 1))
            for n in range(FB * 4, FB * 4 + 4):
                c = n % 4
                wait_slot(n)
                sp.dma_start(wst[:, c, 0], t["l1_wq"][c * P:(c + 1) * P, :]).then_inc(w_ld, 16)
                k, half = divmod(c, 2)
                sp.dma_start(wst[:, c, 1], t["l1_wkv"][k * P:(k + 1) * P, half * 512:(half + 1) * 512]).then_inc(w_ld, 16)
                sp.wait_ge(w_ld, 32 * (n + 1))

            sp.wait_ge(f2_free, 1 + 4 * B * FB)
            sp.wait_ge(w_lo, 2 * 4 * (FB + 1))
            with sp.Fori(0, B) as b:
                sp.wait_ge(dt_lo, 1 + b)
                sp.dma_start(dt_[:], t["ctx"][b].rearrange("(k p) n -> p k n", p=P)).then_inc(dt_ld, 16)

            def max_rows(it, q):
                sp.wait_ge(v_free, V_NUMBER["R", q, 0] + 1 + (V_PER * it if it is not None else 0))
                for pr in range(PAIRS):
                    for hp in range(2):
                        row = 4 * pr + 2 * hp
                        sp.dma_start(f32(qst[64 * hp + ROW_MAX:64 * hp + ROW_MAX + 2, q % RING, pr, :]),
                                     mrow[row:row + 2, q % 2, :]).then_inc(mx_dma, 16)

            sp.wait_ge(q_ready, 1 + 16 * B)
            for s in C2_HEAD:
                for kind, q, _ in attention_step(s):
                    if kind == "R":
                        max_rows(None, q)
            with sp.Fori(0, C2_LOOPS) as it:
                for j in range(C2_BODY):
                    max_rows(it, 2 + j)
            sp.wait_ge(stg_done, NQ)
            sp.dma_start(wraw[:], t["l1_wout"].rearrange("(k p) n -> p k n", p=P)).then_inc(cw_ld, 16)
            for s in C2_TAIL:
                for kind, q, _ in attention_step(s):
                    if kind == "R":
                        max_rows(None, q)
            sp.wait_ge(cw_hi, 1)
            sp.wait_ge(cw_lo, 1)
            sp.dma_start(wraw[:], t["l1_wt"].rearrange("(k p) n -> p k n", p=P)).then_inc(cw_ld, 16)
            sp.wait_ge(va_done, NQ)
            sp.wait_ge(v_free, len(V_NUMBER))
            sp.dma_start(boutb[:], t["bout"]).then_inc(ld_cb, 16)
            sp.dma_start(biasb[:], t["bias"]).then_inc(ld_cb, 16)
            for b in range(B):
                sp.wait_ge(o_free, o_first(b + 1) + 16 if b < B - 1 else 16 * B)
                sp.dma_start(t["out"][b].rearrange("(i p) d -> p i d", p=P), x[:, b * NT:(b + 1) * NT, :]).then_inc(st_out, 16)
            sp.wait_ge(st_out, 16 * B)

        @block.tensor
        def _(pe):
            def transposes(dst_bank, src, rows=P):
                for i in range(NT):
                    last = pe.transpose(dst_bank[0:rows, i * P:(i + 1) * P], src(i), ident[:])
                return last

            def product(dst, terms):
                for n, (a_, b_) in enumerate(terms):
                    last = pe.matmul(dst, a_, b_, start=(n == 0), stop=(n == len(terms) - 1))
                return last

            pe.wait_ge(ld_const, 16 * N_CONST)
            pe.wait_ge(wqk_lo, 1)
            pe.wait_ge(wqk_hi, 1)

            def a_bank(n0, n):
                first = n0 + n - A_RING + 1
                if not isinstance(first, int) or first > 0:
                    pe.wait_ge(a_free, first)
                return bank[a_slot(n0, n)]

            def qk_energy(b, n0, n):
                pe.wait_ge(ct_hi, b + 1)
                pe.wait_ge(ct_lo, b + 1)
                for j in range(2):
                    product(a_bank(n0, n + j), [m for k in range(KC) for m in three(
                        wqkh[:, j, k, :], wqkl[:, j, k, :], cth[:, k, :], ctl[:, k, :])]).then_inc(a_ready, 1)
                pe.wait_ge(a_free, n0 + n + 2)
                for i in range(NT):
                    rows = slice(i * P, (i + 1) * P)
                    if not isinstance(b, int):
                        pe.wait_ge(e_exp, NT * b)
                    product(bank[E_BANK + i], three(qh[:, rows], ql[:, rows], kh[:], kl[:])).then_inc(e_ready, 1)

            def transposed(src, ready, value, n0, n):
                pe.wait_ge(ready, value)
                for k in range(KF):
                    transposes(a_bank(n0, n + k), lambda i: src[:, i, k * P:(k + 1) * P]).then_inc(a_ready, 1)

            def ln_att(n0):
                pe.wait_ge(a_free, n0)
                for i in range(NT):
                    rows = slice(i * P, (i + 1) * P)
                    product(a_bank(n0, i), [m for k in range(NT) for m in three(
                        xth[:, k, rows], xtl[:, k, rows], atth[:, k, :], attl[:, k, :])]).then_inc(a_ready, 1)

            qk_energy(0, 0, 0)
            transposed(xn1, ln_xn, 1 + NT, 0, 2)
            transposed(att, e_att, NT, 0, 6)
            with pe.Fori(0, B - 1) as j:
                n0 = a_first(j)
                ln_att(n0)
                qk_energy(j + 1, n0, 4)
                transposed(xn1, ln_xn, 1 + NT * (2 * j + 2), n0, 6)
                transposed(xn2, ln_xn, 1 + NT * (2 * j + 3), n0, 10)
                transposed(att, e_att, NT * (j + 2), n0, 14)
            n0 = a_first(B - 1)
            ln_att(n0)
            transposed(xn2, ln_xn, 1 + NT * 2 * B, n0, 4)

            pe.wait_ge(a_free, a_first(B - 1) + 8)
            pe.wait_ge(e_exp, NT * B)
            for fb in range(FB):
                par = fb % 2
                pe.wait_ge(w_hi, 8 * (fb + 1))
                pe.wait_ge(w_lo, 8 * (fb + 1))
                with pe.Fori(0, B) as b:
                    it = b + fb * B
                    for f in range(4):
                        pe.wait_ge(f1_gelu, 1 + 4 * it)
                        cols = slice(f * P, (f + 1) * P)
                        product(bank[f], [m for k in range(KF) for m in three(
                            w1h[par][:, k, cols], w1l[par][:, k, cols],
                            x2h[:, bass.ds(b, 1), k, :].rearrange("p o n -> p (o n)"),
                            x2l[:, bass.ds(b, 1), k, :].rearrange("p o n -> p (o n)"))]).then_inc(f1_ready, 1)
                    pe.wait_ge(f2_free, 1 + 4 * it)
                    for f in range(4):
                        pe.wait_ge(g_hi, 1 + 4 * it + f + 1)
                        pe.wait_ge(g_lo, 1 + 4 * it + f + 1)
                        for i in range(NT):
                            rows = slice(i * P, (i + 1) * P)
                            terms = three(gh[:, f, rows], gl[:, f, rows], w2h[par][:, f, :], w2l[par][:, f, :])
                            for n, (a_, b_) in enumerate(terms):
                                last = pe.matmul(bank[4 + i], a_, b_, start=(f == 0 and n == 0),
                                                 stop=(f == 3 and n == 2))
                            if f == 3:
                                last.then_inc(f2_ready, 1)

            pe.wait_ge(f2_free, 1 + 4 * B * FB)
            pe.wait_ge(w_hi, 8 * (FB + 1))
            pe.wait_ge(w_lo, 8 * (FB + 1))
            with pe.Fori(0, B) as b:
                def keys_values(half, i):
                    rows = slice(i * P, (i + 1) * P)
                    cols = slice(half * D, (half + 1) * D)
                    product(bank[i], [m for k in range(KC) for m in three(
                        dth[:, k, rows], dtl[:, k, rows], wkvh[:, k, cols], wkvl[:, k, cols])]).then_inc(q_ready, 1)

                pe.wait_ge(dt_hi, b + 1)
                pe.wait_ge(dt_lo, 1 + b + 1)
                for i in range(NT):
                    pe.wait_ge(v_copied, 4 * b + i + 1)
                    keys_values(0, i)
                pe.wait_ge(ln_xn, 1 + NT * (2 * B + b + 1))
                for k in range(KF):
                    pe.wait_ge(q_free, 12 * b + k + 1)
                    transposes(bank[4 + k], lambda i: tok[:, i, k * P:(k + 1) * P]).then_inc(q_ready, 1)
                for i in range(NT):
                    pe.wait_ge(q_free, 4 + 12 * b + i + 1)
                    keys_values(1, i)
                pe.wait_ge(q_free, 4 + 12 * b + 8)
                for i in range(NT):
                    rows = slice(i * P, (i + 1) * P)
                    product(bank[4 + i], [m for k in range(KF) for m in three(
                        yth[:, k, rows], ytl[:, k, rows], wqh[:, k, :], wql[:, k, :])]).then_inc(q_ready, 1)

            def event(it, kind, q, n):
                def wait(sem_, first, per):
                    if it is not None:
                        pe.wait_ge(sem_, first + per * it)
                    elif first > 0:
                        pe.wait_ge(sem_, first)

                def v_bank():
                    number = V_NUMBER[kind, q, n]
                    wait(v_free, number - 1, V_PER)
                    return bank[6 + number % 2]

                ring = q % RING
                if kind == "S":
                    pr, what = divmod(n, 2)
                    if n == 0:
                        wait(stg_done, q + 1, C2_BODY)
                    wait(s_done, 4 * q + n, 4 * C2_BODY)
                    transposes(bank[5], lambda i: stg[:, q % 2, what, i, 2 * pr:2 * pr + 2, :].rearrange(
                        "p h r -> p (h r)")).then_inc(s_ready, 1)
                elif kind == "M":
                    i, h = divmod(n, 4)
                    if n == 0:
                        wait(s_done, 4 * (q + 1), 4 * C2_BODY)
                    r = 64 * (h % 2)
                    pe.matmul(v_bank(), qst[r:r + 64, ring, h // 2, i * P:(i + 1) * P],
                              kst[r:r + 64, ring, h // 2, :], start=True, stop=True).then_inc(v_ready, 1)
                elif kind == "R":
                    wait(nm_lo, q + 1, C2_BODY)
                    transposes(v_bank(), lambda i: nms[:, i].rearrange("p h s -> p (h s)"), rows=8).then_inc(v_ready, 1)
                elif kind == "QK":
                    kt, pr = divmod(n, 2)
                    gi = 8 * q + n
                    if n == 0:
                        wait(mx_dma, 64 * (q + 1), 64 * C2_BODY)
                    wait(exp_done, gi - 1, 8 * C2_BODY)
                    for hp in range(2):
                        r = 64 * hp
                        last = pe.matmul(bank[2 * (gi % 2) + hp], kst[r:r + 64, ring, pr, kt * P:(kt + 1) * P],
                                         qst[r:r + 64, ring, pr, :], start=True, stop=True)
                    last.then_inc(lt_ready, 1)
                elif kind == "AV":
                    if n == 0:
                        wait(ot_done, q, C2_BODY)
                        wait(va_done, q + 1, C2_BODY)
                    wait(exp_done, 8 * q + 2 * n + 2, 8 * C2_BODY)
                    for h in range(4):
                        gi = 8 * q + 2 * n + h // 2
                        last = pe.matmul(bank[4][32 * h:32 * h + HD + 1, :], va[:, q % 2, n, h, :],
                                         wt[:, gi % 4, h % 2, :], start=(n == 0), stop=(n == NT - 1))
                    last.then_inc(av_done, 1)
                else:
                    wait(ot_done, q + 1, C2_BODY)
                    transposes(v_bank(), lambda i: ots[:, i * P:(i + 1) * P]).then_inc(v_ready, 1)

            pe.wait_ge(q_free, 4 + 12 * B)
            pe.wait_ge(v_copied, 4 + 4 * B)
            pe.wait_ge(ot_init, 1)
            for s in C2_HEAD:
                for ev in attention_step(s):
                    event(None, *ev)
            with pe.Fori(0, C2_LOOPS) as it:
                for j in range(C2_BODY):
                    for ev in attention_step(1 + j):
                        event(it, *ev)
            for s in C2_TAIL:
                if s == C2_TAIL[2]:
                    pe.wait_ge(tn_sum, 1)
                    pe.wait_ge(s_done, 4 * NQ)
                    pe.wait_ge(ones_set, 1)
                    pe.matmul(bank[5][:, 0:2], ones, scl[:, 0:2], start=True, stop=True).then_inc(tn_all, 1)
                for ev in attention_step(s):
                    event(None, *ev)

            pe.wait_ge(cw_hi, 2)
            pe.wait_ge(cw_lo, 1)
            pe.wait_ge(exp_done, 8 * NQ)
            pe.wait_ge(ot_done, NQ)
            pe.wait_ge(v_free, len(V_NUMBER))

            def transpose_att(b):
                pe.wait_ge(at_copy, b + 1)
                for k in range(KF):
                    transposes(bank[k], lambda i: atok[:, i, k * P:(k + 1) * P]).then_inc(o_ready, 1)

            def transpose_ln(b):
                pe.wait_ge(ln_xn, 1 + NT * (3 * B + b + 1))
                for k in range(KF):
                    transposes(bank[4 + k], lambda i: ftok[:, i, k * P:(k + 1) * P]).then_inc(o_ready, 1)

            def out_projection(freed):
                pe.wait_ge(o_free, freed)
                for i in range(NT):
                    rows = slice(i * P, (i + 1) * P)
                    product(bank[i], [m for k in range(KF) for m in three(
                        ath[:, k, rows], atl[:, k, rows], woh[:, k, :], wol[:, k, :])]).then_inc(o_ready, 1)

            def feed_forward(freed):
                pe.wait_ge(o_free, freed)
                for i in range(NT):
                    rows = slice(i * P, (i + 1) * P)
                    product(bank[4 + i], [m for k in range(KF) for m in (
                        (fth[:, k, rows], tern[:, k, :]), (ftl[:, k, rows], tern[:, k, :]))]).then_inc(o_ready, 1)

            transpose_att(0)
            out_projection(KF)
            with pe.Fori(1, B) as b:
                n0 = o_first(b)
                pe.wait_ge(ln_agg, NT * (3 * B + b))
                transpose_att(b)
                pe.wait_ge(o_free, n0)
                transpose_ln(b - 1)
                out_projection(n0 + 4)
                feed_forward(n0 + 8)
            pe.wait_ge(o_free, 16 * B - 8)
            transpose_ln(B - 1)
            feed_forward(16 * B - 4)

        @block.scalar
        def _(act):
            act.wait_ge(ld_const, 16 * N_CONST)
            act.activation(wqkh[:], wqk[:], ACT.Copy).then_inc(wqk_hi, 1)

            def split_ct(b):
                act.wait_ge(ld_ct, 16 * (b + 1))
                act.activation(cth[:], ct[:], ACT.Copy).then_inc(ct_hi, 1)

            def a_group(n0, n):
                act.wait_ge(a_ready, n0 + n + 1)
                return bank[a_slot(n0, n)]

            def softmax(b, n0, n):
                for j, dst in enumerate((qh, kh)):
                    act.activation(dst[:], a_group(n0, n + j), ACT.Identity, bias=bqk[:, j:j + 1]).then_inc(a_hi, 1)
                for i in range(NT):
                    act.wait_ge(e_max, NT * b + i + 1)
                    act.activation(att[:, i, :], bank[E_BANK + i], ACT.Exp, bias=nmax[:, i:i + 1],
                                   accum_out=rsum[:, i:i + 1]).then_inc(e_exp, 1)

            def hi_parts(dst, n0, n):
                for k in range(KF):
                    act.activation(dst(k), a_group(n0, n + k), ACT.Copy).then_inc(a_hi, 1)

            def router_exp(b):
                act.wait_ge(rt_z, NT * (b + 1))
                act.activation(small[:, NT:2 * NT], small[:, 0:NT], ACT.Exp, scale=-1.0,
                               bias=minus_rb[:, 0:1]).then_inc(rt_exp, 1)

            split_ct(0)
            softmax(0, 0, 0)
            hi_parts(lambda k: xth[:, k, :], 0, 2)
            hi_parts(lambda k: atth[:, k, :], 0, 6)
            with act.Fori(0, B - 1) as j:
                n0 = a_first(j)
                act.wait_ge(e_ready, NT * (j + 1))
                split_ct(j + 1)
                softmax(j + 1, n0, 4)
                hi_parts(lambda k: xth[:, k, :], n0, 6)
                hi_parts(lambda k: x2h[:, bass.ds(j, 1), k, :].rearrange("p o n -> p (o n)"), n0, 10)
                hi_parts(lambda k: atth[:, k, :], n0, 14)
                router_exp(j)
            hi_parts(lambda k: x2h[:, B - 1, k, :], a_first(B - 1), 4)
            router_exp(B - 1)
            act.wait_ge(tab, 8)
            for n, dst in ((0, cosd), (1, sind)):
                a_ = ang[:, n].rearrange("p t a f -> p t (a f)")
                act.activation(dst[:, :, :, 0], a_, ACT.Sin, scale=1.0 if n == 0 else -1.0).then_inc(tab_sin, 1)
                act.activation(dst[:, :, :, 1], a_, ACT.Sin).then_inc(tab_sin, 1)

            act.wait_ge(a_free, a_first(B - 1) + 8)
            act.wait_ge(x_b2, NT * B)
            act.wait_ge(tab_sin, 4)
            for fb in range(FB):
                with act.Fori(0, B) as b:
                    it = b + fb * B
                    act.wait_ge(g_lo, 1 + 4 * it)
                    act.wait_ge(g_hi, 1 + 4 * it)
                    for f in range(4):
                        act.wait_ge(f1_ready, 4 * it + f + 1)
                        act.activation(g[:, f, :], bank[f], ACT.Gelu_apprx_tanh,
                                       bias=b1[:, 4 * fb + f:4 * fb + f + 1]).then_inc(f1_gelu, 1)

            act.wait_ge(f2_free, 1 + 4 * B * FB)
            def split_dt(b):
                act.wait_ge(dt_ld, 16 * (b + 1))
                act.activation(dth[:], dt_[:], ACT.Copy).then_inc(dt_hi, 1)

            def c1_batch(b, more):
                for k in range(KF):
                    act.wait_ge(q_ready, 1 + 16 * b + 4 + k + 1)
                    act.activation(yth[:, k, :], bank[4 + k], ACT.Copy).then_inc(q_hi, 1)
                for i in range(NT):
                    act.wait_ge(q_ready, 1 + 16 * b + 8 + i + 1)
                    act.activation(vr[:, bass.ds(QUADS * b, QUADS), i, :],
                                   bank[i].rearrange("p (q n) -> p q n", q=QUADS), ACT.Copy).then_inc(v_copied, 1)
                if more:
                    split_dt(b + 1)

            split_dt(0)
            with act.Fori(0, B - 1) as b:
                c1_batch(b, True)
            c1_batch(B - 1, False)

            def event(it, kind, q, n):
                def wait(sem_, first, per):
                    if it is not None:
                        act.wait_ge(sem_, first + per * it)
                    elif first > 0:
                        act.wait_ge(sem_, first)

                if kind == "S":
                    pr, what = divmod(n, 2)
                    wait(lt_ready, 8 * (q - RING + 1), 8 * C2_BODY)
                    wait(s_ready, 4 * q + n + 1, 4 * C2_BODY)
                    act.activation((qst, kst)[what][:, q % RING, pr, :], bank[5], ACT.Copy).then_inc(s_done, 1)
                elif kind == "QK":
                    gi = 8 * q + n
                    wait(lt_ready, gi + 1, 8 * C2_BODY)
                    wait(av_done, (gi - 4) // 2 + 1, 4 * C2_BODY)
                    two = 2 * (gi % 2)
                    act.activation(wt[:, gi % 4, :, :], banks[:, two:two + 2, :], ACT.Exp,
                                   scale=float(HD) ** -0.5).then_inc(exp_done, 1)
                elif kind == "AV" and n == NT - 1:
                    wait(av_done, 4 * (q + 1), 4 * C2_BODY)
                    if q > 0:
                        wait(v_ready, V_NUMBER["O", q - 1, 0] + 1, V_PER)
                    elif it is not None:
                        wait(v_ready, V_NUMBER["O", q - 1 + C2_BODY, 0] + 1 - V_PER, V_PER)
                    act.activation(ots[:], bank[4], ACT.Copy).then_inc(ot_done, 1)

            act.wait_ge(q_free, 4 + 12 * B)
            for s in C2_HEAD:
                for ev in attention_step(s):
                    event(None, *ev)
            with act.Fori(0, C2_LOOPS) as it:
                for j in range(C2_BODY):
                    for ev in attention_step(1 + j):
                        event(it, *ev)
            for s in C2_TAIL:
                for ev in attention_step(s):
                    event(None, *ev)

            def copy_att(b):
                act.activation(atok[:].rearrange("p i (q n) -> p i q n", q=QUADS),
                               qr[:, bass.ds(QUADS * b, QUADS), :, :].rearrange("p q i n -> p i q n"),
                               ACT.Copy).then_inc(at_copy, 1)

            def hi_o(dst, n0, first_bank):
                for k in range(KF):
                    act.wait_ge(o_ready, n0 + k + 1)
                    act.activation(dst[:, k, :], bank[first_bank + k], ACT.Copy).then_inc(o_hi, 1)

            act.wait_ge(v_free, len(V_NUMBER))
            copy_att(0)
            hi_o(ath, 0, 0)
            copy_att(1)
            with act.Fori(1, B - 1) as b:
                hi_o(ath, o_first(b), 0)
                hi_o(fth, o_first(b) + 4, 4)
                copy_att(b + 1)
            hi_o(ath, o_first(B - 1), 0)
            hi_o(fth, o_first(B - 1) + 4, 4)
            hi_o(fth, 16 * B - 8, 4)

        @block.vector
        def _(dve):
            def ln_statistics(n, b):
                for i in range(NT):
                    dve.bn_stats(stats[:, i, :], tile_of(b, i)).then_inc(ln_stats, 1)
                for i in range(NT):
                    if isinstance(n, int):
                        dve.wait_ge(ln_stats, NT * n + i + 1)
                    else:
                        wait_apart(dve, ln_stats, NT * n + i + 1)
                    dve.bn_aggr(mv[:, i, :], stats[:, i, :]).then_inc(ln_agg, 1)

            def ln_apply(n, b, dst):
                dve.wait_ge(ln_rstd, n + 1)
                for i in range(NT):
                    dve.tensor_scalar(dst[:, i, :], tile_of(b, i), mv[:, i, 0:1], rstd[:, i:i + 1],
                                      ALU.subtract, ALU.mult).then_inc(ln_xn, 1)

            def a_bank(n0, n):
                return bank[a_slot(n0, n)]

            def low_parts(dst, dst_hi, n0, n, h0, h):
                for k in range(KF):
                    dve.wait_ge(a_hi, h0 + h + k + 1)
                    dve.tensor_tensor(dst(k), a_bank(n0, n + k), f32(dst_hi(k)), ALU.subtract).then_inc(a_free, 1)

            def low_qk(n0, n, h0, h):
                for j, (dst, dst_hi) in enumerate(((ql, qh), (kl, kh))):
                    dve.wait_ge(a_hi, h0 + h + j + 1)
                    dve.scalar_tensor_tensor(dst[:], a_bank(n0, n + j), bqk[:, j:j + 1], f32(dst_hi[:]),
                                             ALU.add, ALU.subtract).then_inc(a_free, 1)

            def maxima(b):
                for i in range(NT):
                    dve.wait_ge(e_ready, NT * b + i + 1)
                    dve.tensor_reduce(nmax[:, i:i + 1], bank[E_BANK + i], AX.X, ALU.max, negate=True).then_inc(e_max, 1)

            def normalise(b):
                for i in range(NT):
                    dve.wait_ge(e_exp, NT * b + i + 1)
                    dve.reciprocal(small[:, 12 + i:13 + i], rsum[:, i:i + 1]).then_inc(e_rec, 1)
                for i in range(NT):
                    dve.wait_ge(e_rec, NT * b + i + 1)
                    dve.tensor_scalar(att[:, i, :], att[:, i, :], small[:, 12 + i:13 + i], None, ALU.mult).then_inc(e_att, 1)

            def add_att(b, n0):
                for i in range(NT):
                    dve.wait_ge(a_ready, n0 + i + 1)
                    dve.tensor_tensor(tile_of(b, i), a_bank(n0, i), tile_of(b, i), ALU.add).then_inc(a_free, 1)
                if isinstance(b, int):
                    dve.wait_ge(a_free, n0 + NT)
                else:
                    wait_apart(dve, a_free, n0 + NT)

            def router_scores(b):
                dve.wait_ge(ln_xn, 1 + NT * (2 * b + 3) if not isinstance(b, int) else 1 + NT * 2 * B)
                for i in range(NT):
                    if i:
                        dve.wait_ge(rt_z, NT * b + i)
                    dve.tensor_tensor_reduce(scratch[:], xn2[:, i, :], rw[:], 1.0, 0.0, ALU.mult, ALU.add,
                                             small[:, i:i + 1]).then_inc(rt_z, 1)

            def router_weight(b):
                dve.wait_ge(rt_exp, b + 1)
                dve.tensor_scalar(small[:, 2 * NT:3 * NT], small[:, NT:2 * NT], 1.0, None, ALU.add).then_inc(rt_den, 1)
                dve.wait_ge(rt_den, b + 1)
                dve.reciprocal(router[:, bass.ds(NT * b, NT)], small[:, 2 * NT:3 * NT]).then_inc(rt_w, 1)
                dve.wait_ge(rt_w, b + 1)
                for i in range(NT):
                    dve.wait_ge(x_res, NT * b + i + 1)
                    dve.scalar_tensor_tensor(tile_of(b, i), b2[:], router[:, bass.ds(NT * b + i, 1)], tile_of(b, i),
                                             ALU.mult, ALU.add).then_inc(x_b2, 1)

            dve.wait_ge(ld_const, 16 * N_CONST)
            dve.tensor_scalar(minus_rb[:], rb[:], -1.0, None, ALU.mult)
            dve.wait_ge(ld_x, 16)
            ln_statistics(0, 0)
            ln_apply(0, 0, xn1)
            low_qk(0, 0, 0, 0)
            maxima(0)
            low_parts(lambda k: xtl[:, k, :], lambda k: xth[:, k, :], 0, 2, 0, 2)
            normalise(0)
            low_parts(lambda k: attl[:, k, :], lambda k: atth[:, k, :], 0, 6, 0, 6)
            with dve.Fori(0, B - 1) as j:
                n0, h0 = a_first(j), hi_first(j)
                wait_apart(dve, ld_x, 16 * (j + 2))
                ln_statistics(2 * j + 1, j + 1)
                ln_apply(2 * j + 1, j + 1, xn1)
                add_att(j, n0)
                ln_statistics(2 * j + 2, j)
                low_qk(n0, 4, h0, 0)
                ln_apply(2 * j + 2, j, xn2)
                maxima(j + 1)
                low_parts(lambda k: xtl[:, k, :], lambda k: xth[:, k, :], n0, 6, h0, 2)
                router_scores(j)
                normalise(j + 1)
                x2_j = lambda m: (lambda k: m[:, bass.ds(j, 1), k, :].rearrange("p o n -> p (o n)"))
                low_parts(x2_j(x2l), x2_j(x2h), n0, 10, h0, 6)
                low_parts(lambda k: attl[:, k, :], lambda k: atth[:, k, :], n0, 14, h0, 10)
                router_weight(j)
            last = B - 1
            n0, h0 = a_first(last), hi_first(last)
            add_att(last, n0)
            ln_statistics(2 * B - 1, last)
            ln_apply(2 * B - 1, last, xn2)
            router_scores(last)
            low_parts(lambda k: x2l[:, last, k, :], lambda k: x2h[:, last, k, :], n0, 4, h0, 0)
            router_weight(last)

            two_pi = 2 * np.pi
            c1 = 6.28125
            c2 = float(np.round((two_pi - c1) * 2.0 ** 20)) / 2.0 ** 20
            c3 = two_pi - c1 - c2
            magic = 1.5 * 2.0 ** 23
            freqs = (np.float32(ROPE_BASE) ** (-np.arange(HALF, dtype=np.float32) / np.float32(HALF))).astype(np.float32)
            for f in range(HALF):
                last_ = dve.tensor_scalar(ang[:, 1, :, :, f], pos[:], float(freqs[f]), None, ALU.mult)
            last_.then_inc(tab, 1)
            dve.wait_ge(tab, 1)
            dve.tensor_scalar(ang[:, 0], ang[:, 1], float(np.pi / 2), None, ALU.add).then_inc(tab, 1)
            dve.wait_ge(tab, 2)
            both = ang[:, 0:2].rearrange("p n t a f -> p (n t a f)")
            dve.tensor_scalar(turns[:], both, 1.0 / two_pi, magic, ALU.mult, ALU.add).then_inc(tab, 1)
            dve.wait_ge(tab, 3)
            dve.tensor_scalar(turns[:], turns[:], magic, None, ALU.subtract).then_inc(tab, 1)
            for n, c in enumerate((c1, c2, c3)):
                dve.wait_ge(tab, 4 + n)
                dve.scalar_tensor_tensor(both, turns[:], -c, both, ALU.mult, ALU.add).then_inc(tab, 1)
            dve.wait_ge(tab, 7)
            dve.tensor_scalar(both, both, 3.1415925, -3.1415925, ALU.min, ALU.max).then_inc(tab, 1)

            dve.wait_ge(x_b2, NT * B)
            dve.wait_ge(tab_sin, 4)
            dve.wait_ge(a_ready, a_first(B - 1) + 8)

            def split_hi(fb, c):
                dve.wait_ge(w_ld, 32 * (4 * fb + c + 1))
                for j, dst in enumerate((w1h, w2h)):
                    dve.tensor_copy(dst[fb % 2][:, bass.ds(c, 1), :], wst[:, bass.ds(c, 1), j, :]).then_inc(w_hi, 1)

            for c in range(4):
                split_hi(0, c)
            for fb in range(FB):
                with dve.Fori(0, B) as b:
                    it = b + fb * B
                    for f in range(4):
                        dve.wait_ge(f1_gelu, 1 + 4 * it + f + 1)
                        dve.tensor_copy(gh[:, f, :], g[:, f, :]).then_inc(g_hi, 1)
                    if fb:
                        dve.wait_ge(f2_ready, 4 * B * fb)
                    split_hi(fb + 1, b)
                    for i in range(NT):
                        dve.wait_ge(f2_ready, 4 * it + i + 1)
                        dve.scalar_tensor_tensor(tile_of(b, i), bank[4 + i], router[:, bass.ds(NT * b + i, 1)],
                                                 tile_of(b, i), ALU.mult, ALU.add).then_inc(f2_free, 1)

            dve.wait_ge(f2_free, 1 + 4 * B * FB)
            dve.wait_ge(w_lo, 8 * (FB + 1))
            ln_statistics(2 * B, 0)
            ln_apply(2 * B, 0, tok)

            def rotate(b, c0, bank0, dst, slot0):
                for i in range(NT):
                    n = slot0 + i
                    dve.wait_ge(q_ready, 1 + 16 * b + c0 + i + 1)
                    dve.wait_ge(rope_done, 1 + 2 * NT * b + max(0, n - 1))
                    z = bank[bank0 + i]
                    cos_i, sin_i = (tb[:, bass.ds(NT * b + i, 1), :, :] for tb in (cosd, sind))
                    dve.tensor_tensor(dst[:, bass.ds(QUADS * b, QUADS), i, :].rearrange("p q (h f) -> p q h f", h=4),
                                      z.rearrange("p (q h f) -> p q h f", q=QUADS, h=4),
                                      cos_i.rearrange("p o f e -> p o (f e)").unsqueeze(1).to_broadcast([P, QUADS, 4, HD]),
                                      ALU.mult)
                    z2 = z.rearrange("p (h f e) -> p h f e", h=H, e=2)
                    r2 = rbuf[:, n % 2, :].rearrange("p (h f e) -> p h f e", h=H, e=2)
                    for e in range(2):
                        last = dve.tensor_tensor(r2[:, :, :, e], z2[:, :, :, 1 - e],
                                                 sin_i[:, :, :, e].to_broadcast([P, H, 2 * HALF]), ALU.mult)
                    last.then_inc(q_free, 1)

            def c1_batch(b, more):
                rotate(b, 0, 0, kr, 0)
                for k in range(KF):
                    dve.wait_ge(q_hi, KF * b + k + 1)
                    dve.tensor_tensor(ytl[:, k, :], bank[4 + k], f32(yth[:, k, :]), ALU.subtract).then_inc(q_free, 1)
                if more:
                    ln_statistics(2 * B + 1 + b, b + 1)
                    ln_apply(2 * B + 1 + b, b + 1, tok)
                rotate(b, 12, 4, qr, NT)

            with dve.Fori(0, B - 1) as b:
                c1_batch(b, True)
            c1_batch(B - 1, False)

            dve.wait_ge(q_ready, 1 + 16 * B)
            dve.wait_ge(v_copied, 4 + 4 * B)
            dve.memset(bank[4], 0.0).then_inc(ot_init, 1)

            def event(it, kind, q, n):
                def wait(sem_, first, per):
                    if it is not None:
                        dve.wait_ge(sem_, first + per * it)
                    elif first > 0:
                        dve.wait_ge(sem_, first)

                if kind not in ("M", "R", "O"):
                    return
                number = V_NUMBER[kind, q, n]
                wait(v_ready, number + 1, V_PER)
                src = bank[6 + number % 2]
                if kind == "M":
                    i, h = divmod(n, 4)
                    dve.tensor_reduce(nmx[:, q % 2, i, h:h + 1], src, AX.X, ALU.max, negate=True).then_inc(v_free, 1)
                    if n == 15:
                        wait(v_free, number + 1, V_PER)
                        dve.tensor_copy(r32(nms[:, :, :, 0]), nmx[:, q % 2]).then_inc(nm_hi, 1)
                        wait(nm_hi, q + 1, C2_BODY)
                        dve.tensor_tensor(nms[:, :, :, 1], nmx[:, q % 2], nms[:, :, :, 0], ALU.subtract).then_inc(nm_lo, 1)
                elif kind == "R":
                    dve.tensor_copy(mrow[:, q % 2, :], src[0:8, :]).then_inc(v_free, 1)
                else:
                    o = src.rearrange("p (i h r) -> p i h r", i=NT, h=4)
                    dve.reciprocal(rinv[:, q % 2], o[:, :, :, HD]).then_inc(o_rinv, 1)
                    wait(o_rinv, q + 1, C2_BODY)
                    dst = qr[:, q, :, :] if it is None else qr[:, bass.ds(q + C2_BODY * it, 1), :, :].rearrange(
                        "p o i n -> p (o i) n")
                    dve.tensor_tensor(dst.rearrange("p i (h d) -> p i h d", h=4), o[:, :, :, 0:HD],
                                      rinv[:, q % 2].unsqueeze(3).to_broadcast([P, NT, 4, HD]), ALU.mult).then_inc(v_free, 1)

            for s in C2_HEAD:
                for ev in attention_step(s):
                    event(None, *ev)
            with dve.Fori(0, C2_LOOPS) as it:
                for j in range(C2_BODY):
                    for ev in attention_step(1 + j):
                        event(it, *ev)
            wlin = wraw[:].rearrange("p k n -> p (k n)")
            tlin = tern[:].rearrange("p k n -> p (k n)")
            for s in C2_TAIL:
                if s == C2_TAIL[1]:
                    dve.wait_ge(cw_ld, 16)
                    dve.tensor_copy(woh[:].rearrange("p k n -> p (k n)"), wlin).then_inc(cw_hi, 1)
                if s == C2_TAIL[2]:
                    dve.wait_ge(cw_ld, 32)
                    dve.memset(scl[:, 1:2], 0.0)
                    dve.tensor_reduce(scl[:, 0:1], wlin, AX.X, ALU.add, apply_absolute_value=True).then_inc(tn_sum, 1)
                if s == C2_TAIL[3]:
                    dve.wait_ge(tn_all, 1)
                    dve.tensor_scalar(scl[:, 2:3], bank[5][:, 0:1], 1.0 / (D * D), TERNARY_EPS, ALU.mult, ALU.add)
                    dve.tensor_scalar(scl[:, 3:4], bank[5][:, 0:1], -1.0 / (D * D), None, ALU.mult).then_inc(tn_scale, 1)
                    dve.wait_ge(tn_scale, 1)
                    dve.tensor_scalar(scl[:, 0:1], scl[:, 2:3], 0.5, None, ALU.mult)
                    dve.tensor_scalar(scl[:, 1:2], scl[:, 2:3], -0.5, None, ALU.mult).then_inc(tn_done, 1)
                    dve.wait_ge(tn_done, 1)
                    dve.tensor_scalar(tlin, wlin, scl[:, 0:1], None, ALU.is_gt).then_inc(tn_done, 1)
                    dve.wait_ge(tn_done, 2)
                    dve.scalar_tensor_tensor(tlin, wlin, scl[:, 1:2], f32(tlin), ALU.is_lt, ALU.subtract).then_inc(cw_hi, 1)
                for ev in attention_step(s):
                    event(None, *ev)

            def low_o(dst, dst_hi, h, first_bank):
                for k in range(KF):
                    dve.wait_ge(o_hi, h + k + 1)
                    dve.tensor_tensor(dst[:, k, :], bank[first_bank + k], f32(dst_hi[:, k, :]), ALU.subtract).then_inc(o_free, 1)

            def add_out(b, n):
                for i in range(NT):
                    dve.wait_ge(bo_done, NT * b + i + 1)
                    dve.wait_ge(o_ready, n + i + 1)
                    dve.tensor_tensor(tile_of(b, i), bank[i], tile_of(b, i), ALU.add).then_inc(o_free, 1)

            def normed(b, n):
                if isinstance(b, int):
                    dve.wait_ge(o_free, n)
                else:
                    wait_apart(dve, o_free, n)
                ln_statistics(3 * B + b, b)
                ln_apply(3 * B + b, b, ftok)

            def add_ff(b, n):
                for i in range(NT):
                    dve.wait_ge(x_bias, NT * b + i + 1)
                    dve.wait_ge(o_ready, n + i + 1)
                    dve.scalar_tensor_tensor(tile_of(b, i), bank[4 + i], scl[:, 3:4], tile_of(b, i),
                                             ALU.mult, ALU.add).then_inc(o_free, 1)

            low_o(atl, ath, 0, 0)
            add_out(0, 4)
            normed(0, 8)
            with dve.Fori(1, B) as b:
                n0 = o_first(b)
                low_o(atl, ath, 8 * b - 4, 0)
                low_o(ftl, fth, 8 * b, 4)
                add_out(b, n0 + 8)
                normed(b, n0 + 12)
                add_ff(b - 1, n0 + 12)
            low_o(ftl, fth, 8 * B - 4, 4)
            add_ff(B - 1, 16 * B - 4)

        @block.gpsimd
        def _(pool):
            def rstd_of(n):
                if isinstance(n, int):
                    pool.wait_ge(ln_agg, NT * (n + 1))
                    pool.wait_ge(ln_xn, 1 + NT * n)
                else:
                    wait_apart(pool, ln_agg, NT * (n + 1))
                    wait_apart(pool, ln_xn, 1 + NT * n)
                pool.tensor_scalar(rstd[:], mv[:, :, 1], LN_EPS, 1.0, ALU.add, ALU.mult).then_inc(ln_eps, 1)
                pool.wait_ge(ln_eps, n + 1)
                pool.tensor_tensor(rstd[:], rstd[:], minus_half[:], ALU.pow).then_inc(ln_rstd, 1)

            pool.wait_ge(ld_const, 16 * N_CONST)
            pool.wait_ge(wqk_hi, 1)
            pool.tensor_tensor(wqkl[:], wqk[:], f32(wqkh[:]), ALU.subtract).then_inc(wqk_lo, 1)

            def split_ct(b):
                pool.wait_ge(ct_hi, b + 1)
                pool.tensor_tensor(ctl[:], ct[:], f32(cth[:]), ALU.subtract).then_inc(ct_lo, 1)

            def residual(b, n):
                for i in range(NT):
                    if isinstance(b, int):
                        pool.wait_ge(ln_xn, 1 + NT * n + i + 1)
                    else:
                        wait_apart(pool, ln_xn, 1 + NT * n + i + 1)
                    pool.tensor_tensor(tile_of(b, i), tile_of(b, i), xn2[:, i, :], ALU.add).then_inc(x_res, 1)

            split_ct(0)
            rstd_of(0)
            with pool.Fori(0, B - 1) as j:
                rstd_of(2 * j + 1)
                split_ct(j + 1)
                rstd_of(2 * j + 2)
                residual(j, 2 * j + 2)
            rstd_of(2 * B - 1)
            residual(B - 1, 2 * B - 1)

            pool.wait_ge(a_ready, a_first(B - 1) + 8)
            pool.wait_ge(tab_sin, 4)

            def split_lo(fb, c):
                if isinstance(c, int):
                    pool.wait_ge(w_hi, 2 * (4 * fb + c + 1))
                else:
                    wait_apart(pool, w_hi, 2 * (4 * fb + c + 1))
                for j, (dst, hi_) in enumerate(((w1l, w1h), (w2l, w2h))):
                    pool.tensor_tensor(dst[fb % 2][:, bass.ds(c, 1), :], wst[:, bass.ds(c, 1), j, :],
                                       f32(hi_[fb % 2][:, bass.ds(c, 1), :]), ALU.subtract).then_inc(w_lo, 1)

            for c in range(4):
                split_lo(0, c)
            for fb in range(FB):
                with pool.Fori(0, B) as b:
                    it = b + fb * B
                    for f in range(4):
                        pool.wait_ge(g_hi, 1 + 4 * it + f + 1)
                        pool.tensor_tensor(gl[:, f, :], g[:, f, :], f32(gh[:, f, :]), ALU.subtract).then_inc(g_lo, 1)
                    split_lo(fb + 1, b)

            pool.wait_ge(f2_free, 1 + 4 * B * FB)
            rstd_of(2 * B)

            def add_rotated(b, c0, dst, slot0):
                for i in range(NT):
                    n = slot0 + i
                    d = dst[:, bass.ds(QUADS * b, QUADS), i, :]
                    if isinstance(b, int):
                        pool.wait_ge(q_free, 4 + 12 * b + c0 + i + 1)
                    else:
                        wait_apart(pool, q_free, 4 + 12 * b + c0 + i + 1)
                    pool.tensor_tensor(d, d, rbuf[:, n % 2, :].rearrange("p (q n) -> p q n", q=QUADS),
                                       ALU.add).then_inc(rope_done, 1)

            def split_dt(b):
                pool.wait_ge(dt_hi, b + 1)
                pool.tensor_tensor(dtl[:], dt_[:], f32(dth[:]), ALU.subtract).then_inc(dt_lo, 1)

            def c1_batch(b, more):
                add_rotated(b, 0, kr, 0)
                if more:
                    rstd_of(2 * B + 1 + b)
                    split_dt(b + 1)
                add_rotated(b, 8, qr, NT)

            split_dt(0)
            with pool.Fori(0, B - 1) as b:
                c1_batch(b, True)
            c1_batch(B - 1, False)

            pool.wait_ge(q_ready, 1 + 16 * B)
            pool.wait_ge(q_free, 4 + 12 * B)
            pool.wait_ge(v_copied, 4 + 4 * B)
            pool.wait_ge(rope_done, 1 + 2 * NT * B)
            pool.memset(ones, 1.0).then_inc(ones_set, 1)
            pool.memset(va[:].rearrange("p r i h d -> p (r i h d)"), 1.0).then_inc(stg_zero, 1)
            for par in range(2):
                pool.memset(stg[:, par, 0, :, :, ROW_MAX:64], 0.0)
                pool.memset(stg[:, par, 1, :, :, ROW_MAX:ROW_MAX + 2], 1.0)
                last = pool.memset(stg[:, par, 1, :, :, ROW_MAX + 2:64], 0.0)
            last.then_inc(stg_zero, 1)

            def stage(it, q):
                def wait(sem_, first, per):
                    if it is not None:
                        wait_apart(pool, sem_, first + per * it)
                    elif first > 0:
                        pool.wait_ge(sem_, first)

                def quad(m):
                    return m[:, q, :, :] if it is None else m[:, bass.ds(q + C2_BODY * it, 1), :, :].rearrange(
                        "p o i n -> p (o i) n")

                wait(s_ready, 4 * (q - 1), 4 * C2_BODY)
                for what, src, lo_at, hi_at in ((0, qr, 1, 2), (1, kr, 2, 1)):
                    sv = stg[:, q % 2, what].rearrange("p i h (j d) -> p i h j d", j=4)
                    src_q = quad(src).rearrange("p i (h d) -> p i h d", h=4)
                    pool.tensor_copy(r32(sv[:, :, :, 0, :]), src_q).then_inc(stg_hi, 1)
                    wait(stg_hi, 2 * q + what + 1, 2 * C2_BODY)
                    pool.tensor_copy(sv[:, :, :, hi_at, :], sv[:, :, :, 0, :])
                    last = pool.tensor_tensor(sv[:, :, :, lo_at, :], src_q, sv[:, :, :, 0, :], ALU.subtract)
                last.then_inc(stg_done, 1)

            def values(it, q):
                if it is not None:
                    wait_apart(pool, av_done, 4 * (q - 1) + 4 * C2_BODY * it)
                elif q >= 2:
                    pool.wait_ge(av_done, 4 * (q - 1))
                src = vr[:, q, :, :] if it is None else vr[:, bass.ds(q + C2_BODY * it, 1), :, :].rearrange(
                    "p o i n -> p (o i) n")
                pool.tensor_copy(va[:, q % 2, :, :, 0:HD], src.rearrange("p i (h d) -> p i h d", h=4)).then_inc(va_done, 1)

            pool.wait_ge(stg_zero, 2)
            for q in range(4):
                stage(None, q)
                if q < 2:
                    values(None, q)
            with pool.Fori(0, C2_LOOPS) as it:
                for j in range(C2_BODY):
                    stage(it, 4 + j)
                    values(it, 2 + j)
            values(None, NQ - 2)
            pool.wait_ge(cw_hi, 1)
            pool.tensor_tensor(wol[:].rearrange("p k n -> p (k n)"), wraw[:].rearrange("p k n -> p (k n)"),
                               f32(woh[:].rearrange("p k n -> p (k n)")), ALU.subtract).then_inc(cw_lo, 1)
            values(None, NQ - 1)

            def add_bout(b):
                for i in range(NT):
                    pool.tensor_tensor(tile_of(b, i), tile_of(b, i), boutb[:], ALU.add).then_inc(bo_done, 1)

            def add_bias(b):
                for i in range(NT):
                    if isinstance(b, int):
                        pool.wait_ge(ln_xn, 1 + NT * (3 * B + b) + i + 1)
                    else:
                        wait_apart(pool, ln_xn, 1 + NT * (3 * B + b) + i + 1)
                    pool.tensor_tensor(tile_of(b, i), tile_of(b, i), biasb[:], ALU.add).then_inc(x_bias, 1)

            pool.wait_ge(v_free, len(V_NUMBER))
            pool.wait_ge(ld_cb, 32)
            add_bout(0)
            rstd_of(3 * B)
            with pool.Fori(1, B) as b:
                add_bout(b)
                add_bias(b - 1)
                rstd_of(3 * B + b)
            add_bias(B - 1)


def layouts(np_, v):
    c = np_.ascontiguousarray

    def over(a):
        return c(np_.broadcast_to(a.reshape(1, -1), (P, a.size)))

    return {
        "x": c(v["x"]),
        "ctx": c(v["ctx_1024"].transpose(0, 2, 1)),
        "pos": c(v["fside_BxSx2_0"].reshape(B * NT, P, 2).transpose(1, 0, 2)),
        "l0_wq": c(v["L0_xattn_Wq"].T),
        "l0_wk": c(v["L0_xattn_Wk"].T),
        "bqk": c(np_.stack([v["L0_xattn_bq"], v["L0_xattn_bk"]], axis=1)),
        "rw": over(v["L0_ffn_router_weight"]),
        "rb": over(v["L0_ffn_router_bias"]),
        "w1": c(v["L0_ffn_w1"]),
        "b1": c(v["L0_ffn_b1"].reshape(DFF // P, P).T),
        "w2": c(v["L0_ffn_w2"]),
        "b2": over(v["L0_ffn_b2"]),
        "l1_wq": c(v["L1_xattn_Wq"]),
        "l1_wkv": c(v["L1_xattn_Wkv"]),
        "l1_wout": c(v["L1_xattn_Wout"]),
        "bout": over(v["L1_xattn_bout"]),
        "l1_wt": c(v["L1_ffn_weight"].T),
        "bias": over(v["L1_ffn_bias"]),
        "ident": np_.eye(P, dtype=np_.float32),
        "minus_half": np_.full((P, NT), -0.5, np_.float32),
    }


def kernel(**inputs):
    import concourse.bacc as bacc
    from concourse.bass_utils import run_bass_kernel_spmd

    arrays = layouts(np, {k: np.asarray(v) for k, v in inputs.items()})
    nc = bacc.Bacc("TRN2", target_bir_lowering=False, num_devices=1)
    t = {k: nc.dram_tensor("in_" + k, a.shape, mybir.dt.from_np(a.dtype), kind="ExternalInput").ap() for k, a in arrays.items()}
    t["out"] = nc.dram_tensor("out", (B, S, D), F32, kind="ExternalOutput").ap()
    build(nc, t)
    arrays = {"in_" + k: a for k, a in arrays.items()}
    return run_bass_kernel_spmd(nc, [arrays], core_ids=[0]).results[0]["out"]
```

```python
from contextlib import ExitStack

import concourse.bass as bass
import concourse.mybir as mybir
import numpy as np

F32 = mybir.dt.float32
F32R = mybir.dt.float32r
ACT = mybir.ActivationFunctionType
ALU = mybir.AluOpType
AX = mybir.AxisListType

P = 128
B, S, D = 4, 512, 512
C = 256
DQK = 128
DFF = 2048
H, HD = 32, 16
NT = S // P
KF = D // P
KC = C // P
FB = DFF // 512
W = 512
LN_EPS = 1e-5
TERNARY_EPS = 1e-10
ROPE_BASE = 10000.0
HALF = 4

QUADS = H // 4
PAIRS = 2
ROW_MAX = 48
RING = 4
NQ = B * QUADS

A_PER = 18
E_BANK = 4


def attention_step(s):
    order = []
    for slot in range(8):
        order.append(("M", s + 2, 2 * slot))
        if slot % 2 == 0:
            order.append(("S", s + 3, slot // 2))
        if slot == 1:
            order.append(("AV", s - 1, NT - 1))
        if slot in (3, 5, 7):
            order.append(("AV", s, slot // 2 - 1))
        order.append(("M", s + 2, 2 * slot + 1))
        order.append(("QK", s, slot))
        if slot == (2 if s + 2 < NQ else 0):
            order.append(("R", s + 1, 0))
        if slot == 4:
            order.append(("O", s - 1, 0))
    return [e for e in order if 0 <= e[1] < NQ]


V_NUMBER = {}
for _s in range(-3, NQ + 1):
    for _e in attention_step(_s):
        if _e[0] in ("M", "R", "O"):
            V_NUMBER[_e] = len(V_NUMBER)
C2_HEAD = range(-3, 1)
C2_BODY = 4
C2_LOOPS = (NQ - 4) // C2_BODY
C2_TAIL = range(1 + C2_BODY * C2_LOOPS, NQ + 1)
V_PER = 18 * C2_BODY


def build(nc, t):
    with ExitStack() as ctx:
        def sb(name, shape, dt=F32, stack=ctx):
            return stack.enter_context(nc.sbuf_tensor(name, shape, dt))

        def sem(name):
            return ctx.enter_context(nc.semaphore(name))

        banks = ctx.enter_context(nc.psum_tensor("banks", [P, 8, W], F32))
        bank = [banks[:, i, :] for i in range(8)]

        x = sb("x", [P, B * NT, D])
        ident = sb("ident_sb", [P, P])
        b1 = sb("b1_sb", [P, DFF // P])
        rb = sb("rb_sb", [P, 1])
        minus_rb = sb("minus_rb", [P, 1])
        router = sb("router", [P, B * NT])
        mv = sb("mv", [P, NT, 2])
        stats = sb("stats", [P, 2, NT, 6])
        rstd = sb("rstd", [P, NT])
        minus_half = sb("minus_half", [P, NT])
        shift = sb("shift", [P, NT])
        small = sb("small", [P, 5 * NT])
        scl = sb("scl", [P, 4])
        cosd = sb("cosd", [P, B * NT, 2 * HALF, 2])
        sind = sb("sind", [P, B * NT, 2 * HALF, 2])
        ones = cosd[:].rearrange("p t f e -> p (t f e)")[:, 0:P]

        ab = ExitStack()
        x2h = sb("x2h", [P, B, KF, S], F32R, ab)
        x2l = sb("x2l", [P, B, KF, S], F32R, ab)
        ph_a = ExitStack()
        ct = sb("ct", [P, KC, S], F32, ph_a)
        cth = sb("cth", [P, KC, S], F32R, ph_a)
        ctl = sb("ctl", [P, KC, S], F32R, ph_a)
        qh, ql, kh, kl = (sb(n, [P, S], F32R, ph_a) for n in ("qh", "ql", "kh", "kl"))
        wqk = sb("wqk", [P, 2, KC, DQK], F32, ph_a)
        wqkh = sb("wqkh", [P, 2, KC, DQK], F32R, ph_a)
        wqkl = sb("wqkl", [P, 2, KC, DQK], F32R, ph_a)
        att = sb("att", [P, NT, S], F32, ph_a)
        xn1 = sb("xn1", [P, NT, D], F32, ph_a)
        sb("phase_a_pad", [P, 3, D], F32, ph_a)
        xn2 = sb("xn2", [P, NT, D], F32, ph_a)
        b2w = sb("b2w", [P, 2, D], F32, ph_a)
        rw = sb("rw_sb", [P, D], F32, ph_a)
        b2 = sb("b2_sb", [P, D], F32, ph_a)
        scratch = sb("scratch", [P, D], F32, ph_a)
        bqk = sb("bqk", [P, 2], F32, ph_a)
        pos = sb("pos_sb", [P, B * NT, 2], F32, ph_a)
        ang = sb("ang", [P, 2, B * NT, 2, HALF], F32, ph_a)
        turns = sb("turns", [P, 2 * B * NT * 2 * HALF], F32, ph_a)
        nmax = sb("nmax", [P, NT], F32, ph_a)
        rsum = sb("rsum", [P, NT], F32, ph_a)
        xth = sb("xth", [P, KF, S], F32R, ph_a)
        xtl = sb("xtl", [P, KF, S], F32R, ph_a)
        atth = sb("atth", [P, NT, S], F32R, ph_a)
        attl = sb("attl", [P, NT, S], F32R, ph_a)
        ph_a.close()

        ph_b = ExitStack()
        even = [sb(n, [P, KF, 512], F32R, ph_b) for n in ("w1h0", "w1l0", "w2h0", "w2l0")]
        wst = sb("wst", [P, 4, 2, 512], F32, ph_b)
        odd = [sb(n, [P, KF, 512], F32R, ph_b) for n in ("w1h1", "w1l1", "w2h1", "w2l1")]
        w1h, w1l, w2h, w2l = zip(even, odd)
        g = sb("g", [P, 4, S], F32, ph_b)
        gh = sb("gh", [P, 4, S], F32R, ph_b)
        gl = sb("gl", [P, 4, S], F32R, ph_b)
        ph_b.close()
        ab.close()

        ctx_place = ExitStack()
        sb("ctx_place", [P, B - 2, KF, S], F32, ctx_place)
        dt_ = sb("dt_", [P, KC, S], F32, ctx_place)
        sb("ctx_pad", [P, KC, S], F32, ctx_place)
        dth = sb("dth", [P, KC, S], F32R, ctx_place)
        dtl = sb("dtl", [P, KC, S], F32R, ctx_place)
        ctx_place.close()
        qr = sb("qr", [P, NQ, NT, 64])
        kr_stack = ExitStack()
        kr = sb("kr", [P, NQ, NT, 64], F32, kr_stack)
        even_place = ExitStack()
        sb("even_place", [P, 4, KF, 512], F32, even_place)
        vr_stack = ExitStack()
        vr = sb("vr", [P, NQ, NT, 64], F32, vr_stack)
        wqh, wql = even[0], even[1]
        wkvh, wkvl = (w[:].rearrange("p k n -> p (k n)").rearrange("p (k n) -> p k n", k=KC) for w in even[2:])
        ph_c1 = ExitStack()
        tok = sb("tok", [P, NT, D], F32, ph_c1)
        yth = sb("yth", [P, KF, S], F32R, ph_c1)
        ytl = sb("ytl", [P, KF, S], F32R, ph_c1)
        rbuf = sb("rbuf", [P, 2, D], F32, ph_c1)
        ph_c1.close()

        ph_c2 = ExitStack()
        qst = sb("qst", [P, RING, PAIRS, S], F32R, ph_c2)
        kst = sb("kst", [P, RING, PAIRS, S], F32R, ph_c2)
        nmx = sb("nmx", [P, 2, NT, 4], F32, ph_c2)
        nms = sb("nms", [P, NT, 4, 2], F32, ph_c2)
        mrow = sb("mrow", [8, 2, S], F32, ph_c2)
        ots = sb("ots", [P, S], F32, ph_c2)
        rinv = sb("rinv", [P, 2, NT, 4], F32, ph_c2)
        va = sb("va", [P, 2, NT, 4, HD + 1], F32, ph_c2)
        ph_c2.close()
        vr_stack.close()
        even_place.close()
        ph_c2 = ExitStack()
        stg = sb("stg", [P, 2, 2, NT, 4, 64], F32, ph_c2)
        wt = sb("wt", [P, 4, 2, S], F32, ph_c2)
        ph_c2.close()
        kr_stack.close()

        woh = sb("woh", [P, KF, D], F32R)
        wol = sb("wol", [P, KF, D], F32R)
        tern = sb("tern", [P, KF, D], F32R)
        wraw = sb("wraw", [P, KF, D])
        atok = sb("atok", [P, NT, D])
        ath = sb("ath", [P, KF, S], F32R)
        atl = sb("atl", [P, KF, S], F32R)
        ftok = sb("ftok", [P, NT, D])
        boutb = sb("bout_sb", [P, D])
        biasb = sb("bias_sb", [P, D])
        fth = sb("fth", [P, KF, S], F32R)
        ftl = sb("ftl", [P, KF, S], F32R)

        STACKS = ((0, qr, 1, 2), (1, kr, 2, 1))

        ld_const, ld_wqk, ld_x, ld_ct = sem("ld_const"), sem("ld_wqk"), sem("ld_x"), sem("ld_ct")
        tab, tab_sin = sem("tab"), sem("tab_sin")
        wqk_hi, wqk_lo = sem("wqk_hi"), sem("wqk_lo")
        ln_stats, ln_agg, ln_eps, ln_pow, ln_rstd, ln_xn = (
            sem("ln_" + n) for n in ("stats", "agg", "eps", "pow", "rstd", "xn"))
        ct_hi, ct_lo = sem("ct_hi"), sem("ct_lo")
        a_ready, a_free, a_hi = sem("a_ready"), sem("a_free"), sem("a_hi")
        e_ready, e_max, e_exp, e_rec, e_att = (sem("e_" + n) for n in ("ready", "max", "exp", "rec", "att"))
        rt_z, rt_exp, rt_den, rt_w, x_res, x_b2 = (sem(n) for n in ("rt_z", "rt_exp", "rt_den", "rt_w", "x_res", "x_b2"))
        w_ld, w_hi, w_lo = sem("w_ld"), sem("w_hi"), sem("w_lo")
        f1_ready, f1_gelu, g_hi, g_lo, f2_ready, f2_free = (sem(n) for n in ("f1_ready", "f1_gelu", "g_hi", "g_lo", "f2_ready", "f2_free"))
        q_ready, q_free, q_hi = sem("q_ready"), sem("q_free"), sem("q_hi")
        dt_ld, dt_hi, dt_lo = sem("dt_ld"), sem("dt_hi"), sem("dt_lo")
        v_copied = sem("v_copied")
        rope_done = sem("rope_done")
        ones_set, stg_zero, stg_hi, stg_done = sem("ones_set"), sem("stg_zero"), sem("stg_hi"), sem("stg_done")
        va_done = sem("va_done")
        v_ready, v_free = sem("v_ready"), sem("v_free")
        s_ready, s_done, lt_ready, exp_done, av_done, ot_done = (
            sem(n) for n in ("s_ready", "s_done", "lt_ready", "exp_done", "av_done", "ot_done"))
        nm_hi, nm_lo, mx_dma, o_rinv = sem("nm_hi"), sem("nm_lo"), sem("mx_dma"), sem("o_rinv")
        ot_init = sem("ot_init")
        cw_ld, cw_hi, cw_lo, ld_cb = sem("cw_ld"), sem("cw_hi"), sem("cw_lo"), sem("ld_cb")
        tn_sum, tn_all, tn_scale, tn_done = (sem("tn_" + n) for n in ("sum", "all", "scale", "done"))
        at_copy, o_ready, o_free, o_hi = sem("at_copy"), sem("o_ready"), sem("o_free"), sem("o_hi")
        first_hi, first_done = sem("first_hi"), sem("first_done")
        b2_w = sem("b2_w")
        bo_done = sem("bo_done")
        x_bias, st_out = sem("x_bias"), sem("st_out")

        block = ctx.enter_context(nc.Block())

        def f32(ap):
            return ap.bitcast(F32)

        def r32(ap):
            return ap.bitcast(F32R)

        STARTED = tuple((s, 1) for s in (f1_gelu, f2_free, g_lo, g_hi, q_ready, rope_done, dt_lo, ln_xn)) + (
            (q_free, 4), (v_copied, 4))

        N_CONST = 8

        def wait_apart(eng, sem_, value):
            value = eng.to_reg(value)
            eng.wait_ge(ld_const, 16 * N_CONST)
            eng.wait_ge(sem_, value)

        def three(ah, al, bh, bl):
            return ((ah, bh), (ah, bl), (al, bh))

        A_HEAD = HI_HEAD = 12
        HI_PER = A_PER - NT

        def a_first(j):
            return A_HEAD + A_PER * j

        def hi_first(j):
            return HI_HEAD + HI_PER * j

        A_TAIL = a_first(B - 2) + A_PER - 2
        HI_TAIL = hi_first(B - 2) + HI_PER - 2
        A_ALL = A_TAIL + 2 * NT

        def xm_bank(i):
            return bank[E_BANK + 2 + i if i < 2 else i]

        def o_first(b):
            return 16 * b - 8

        def v_place(kind, q, n):
            return bank[n % 4] if kind == "M" and q < 2 else bank[6 + V_NUMBER[kind, q, n] % 2]

        def s_bank(q, n):
            return bank[5 if q else n]

        def tile_of(b, i):
            return x[:, bass.ds(NT * b + i, 1), :].rearrange("p o n -> p (o n)")

        @block.sync
        def _(sp):
            for counted, start in STARTED:
                sp.sem_inc(counted, start)
            for j, name in enumerate(("l0_wq", "l0_wk")):
                sp.dma_start(wqk[:, j], t[name].rearrange("(k p) d -> p k d", p=P)).then_inc(ld_wqk, 16)
            sp.dma_start(ct[:], t["ctx"][0].rearrange("(k p) n -> p k n", p=P)).then_inc(ld_ct, 16)
            sp.dma_start(x[:, 0:NT, :], t["x"][0].rearrange("(i p) d -> p i d", p=P)).then_inc(ld_x, 16)
            for dst, name in ((bqk, "bqk"), (ident, "ident"), (minus_half, "minus_half"), (b1, "b1"), (rb, "rb"),
                              (rw, "rw"), (b2, "b2"), (pos, "pos")):
                sp.dma_start(dst[:], t[name]).then_inc(ld_const, 16)
            sp.wait_ge(ld_x, 16)
            for b in range(1, B):
                sp.wait_ge(ct_lo, b)
                sp.dma_start(ct[:], t["ctx"][b].rearrange("(k p) n -> p k n", p=P)).then_inc(ld_ct, 16)
                sp.dma_start(x[:, NT * b:NT * (b + 1), :], t["x"][b].rearrange("(i p) d -> p i d", p=P)).then_inc(ld_x, 16)
                sp.wait_ge(ld_x, 16 * (b + 1))

            sp.wait_ge(a_free, a_first(B - 2) + 12)

            def wait_slot(n):
                if n >= 4:
                    sp.wait_ge(w_hi, 2 * (n - 3))
                    sp.wait_ge(w_lo, 2 * (n - 3))

            for n in range(FB * 4):
                fb, c = divmod(n, 4)
                wait_slot(n)
                sp.dma_start(wst[:, c, 0], t["w1"][c * P:(c + 1) * P, fb * 512:(fb + 1) * 512]).then_inc(w_ld, 16)
                sp.dma_start(wst[:, c, 1], t["w2"][(4 * fb + c) * P:(4 * fb + c + 1) * P, :]).then_inc(w_ld, 16)
                sp.wait_ge(w_ld, 32 * (n + 1))
            for n in range(FB * 4, FB * 4 + 4):
                c = n % 4
                wait_slot(n)
                sp.dma_start(wst[:, c, 0], t["l1_wq"][c * P:(c + 1) * P, :]).then_inc(w_ld, 16)
                k, half = divmod(c, 2)
                sp.dma_start(wst[:, c, 1], t["l1_wkv"][k * P:(k + 1) * P, half * 512:(half + 1) * 512]).then_inc(w_ld, 16)
                sp.wait_ge(w_ld, 32 * (n + 1))

            sp.wait_ge(f1_ready, 4 * B * FB)
            with sp.Fori(0, B) as b:
                sp.wait_ge(dt_lo, 1 + b)
                sp.dma_start(dt_[:], t["ctx"][b].rearrange("(k p) n -> p k n", p=P)).then_inc(dt_ld, 16)

            def max_rows(it, q):
                sp.wait_ge(v_free, V_NUMBER["R", q, 0] + 1 + (V_PER * it if it is not None else 0))
                for pr in range(PAIRS):
                    for hp in range(2):
                        row = 4 * pr + 2 * hp
                        sp.dma_start(f32(qst[64 * hp + ROW_MAX:64 * hp + ROW_MAX + 2, q % RING, pr, :]),
                                     mrow[row:row + 2, q % 2, :]).then_inc(mx_dma, 16)

            sp.wait_ge(q_ready, 1 + 16 * B)
            for s in C2_HEAD:
                for kind, q, _ in attention_step(s):
                    if kind == "R":
                        max_rows(None, q)
            with sp.Fori(0, C2_LOOPS) as it:
                for j in range(C2_BODY):
                    max_rows(it, 2 + j)
            sp.wait_ge(stg_done, NQ - 1)
            sp.dma_start(wraw[:], t["l1_wout"].rearrange("(k p) n -> p k n", p=P)).then_inc(cw_ld, 16)
            for s in C2_TAIL:
                for kind, q, _ in attention_step(s):
                    if kind == "R":
                        max_rows(None, q)
            sp.wait_ge(cw_hi, 1)
            sp.wait_ge(cw_lo, 1)
            sp.dma_start(wraw[:], t["l1_wt"].rearrange("(k p) n -> p k n", p=P)).then_inc(cw_ld, 16)
            sp.wait_ge(va_done, NQ)
            sp.dma_start(boutb[:], t["bout"]).then_inc(ld_cb, 16)
            sp.dma_start(biasb[:], t["bias"]).then_inc(ld_cb, 16)
            for b in range(B - 1):
                sp.wait_ge(o_free, o_first(b + 1) + 16)
                sp.dma_start(t["out"][b].rearrange("(i p) d -> p i d", p=P), x[:, b * NT:(b + 1) * NT, :]).then_inc(st_out, 16)
            for i in range(NT):
                sp.wait_ge(o_free, 16 * B - NT + i + 1)
                sp.dma_start(t["out"][B - 1, i * P:(i + 1) * P, :], x[:, NT * (B - 1) + i, :]).then_inc(st_out, 16)
            sp.wait_ge(st_out, 16 * (B - 1 + NT))

        @block.tensor
        def _(pe):
            def transposes(dst_bank, src, rows=P):
                for i in range(NT):
                    last = pe.transpose(dst_bank[0:rows, i * P:(i + 1) * P], src(i), ident[:])
                return last

            def product(dst, terms):
                for n, (a_, b_) in enumerate(terms):
                    last = pe.matmul(dst, a_, b_, start=(n == 0), stop=(n == len(terms) - 1))
                return last

            pe.wait_ge(wqk_lo, 1)
            pe.wait_ge(wqk_hi, 1)

            def a_freed(n):
                if not isinstance(n, int) or n > 0:
                    pe.wait_ge(a_free, n)

            def queries_keys(b, n0, n):
                pe.wait_ge(ct_hi, b + 1)
                pe.wait_ge(ct_lo, b + 1)
                if not isinstance(b, int) or b:
                    pe.wait_ge(e_exp, NT * b)
                for j in range(2):
                    product(bank[E_BANK + j], [m for k in range(KC) for m in three(
                        wqkh[:, j, k, :], wqkl[:, j, k, :], cth[:, k, :], ctl[:, k, :])]).then_inc(a_ready, 1)

            def energies(b, n, after=True):
                pe.wait_ge(a_free, n)
                for i in range(NT):
                    rows = slice(i * P, (i + 1) * P)
                    if after and i >= 2:
                        a_freed(n + 4 + i - 2 + 1)
                    product(bank[E_BANK + i], three(qh[:, rows], ql[:, rows], kh[:], kl[:])).then_inc(e_ready, 1)

            def transposed(src, ready, value, n0, n, before=NT):
                pe.wait_ge(ready, value)
                for k in range(KF):
                    a_freed(n0 + n + k - before + 1)
                    transposes(bank[k], lambda i: src[:, i, k * P:(k + 1) * P]).then_inc(a_ready, 1)

            def ln_att(b, n0, tiles):
                for i in tiles:
                    rows = slice(i * P, (i + 1) * P)
                    if i < 2:
                        pe.wait_ge(e_exp, NT * (b + 1))
                    else:
                        a_freed(n0 + i - NT + 1)
                    product(xm_bank(i), [m for k in range(NT) for m in three(
                        xth[:, k, rows], xtl[:, k, rows], atth[:, k, :], attl[:, k, :])]).then_inc(a_ready, 1)

            def a_iteration(j, more):
                n0 = a_first(j)
                pe.wait_ge(a_free, n0 - 6)
                ln_att(j, n0, (0, 1))
                energies(j + 1, n0 - 4)
                ln_att(j, n0, (2, 3))
                transposed(xn1, ln_xn, 1 + NT * (2 * j + 2), n0, 4)
                transposed(att, e_att, NT * (j + 2), n0, 8)
                if more:
                    queries_keys(j + 2, n0, 12)
                transposed(xn2, ln_xn, 1 + NT * (2 * j + 3), n0, *((14, 6) if more else (12, 4)))

            queries_keys(0, 0, 0)
            pe.wait_ge(ld_const, 16 * N_CONST)
            energies(0, 2, False)
            transposed(xn1, ln_xn, 1 + NT, 0, 2)
            transposed(att, e_att, NT, 0, 6)
            queries_keys(1, 0, 10)
            pe.wait_ge(a_free, A_HEAD)
            with pe.Fori(0, B - 2) as j:
                a_iteration(j, True)
            a_iteration(B - 2, False)
            pe.wait_ge(a_free, A_TAIL - 4)
            ln_att(B - 1, A_TAIL, range(NT))
            transposed(xn2, ln_xn, 1 + NT * 2 * B, A_TAIL, 4)

            pe.wait_ge(a_free, A_ALL)
            pe.wait_ge(e_exp, NT * B)
            for fb in range(FB):
                par = fb % 2
                pe.wait_ge(w_hi, 8 * (fb + 1))
                pe.wait_ge(w_lo, 8 * (fb + 1))
                with pe.Fori(0, B) as b:
                    it = b + fb * B
                    for f in range(4):
                        pe.wait_ge(f1_gelu, 1 + 4 * it)
                        cols = slice(f * P, (f + 1) * P)
                        product(bank[f], [m for k in range(KF) for m in three(
                            w1h[par][:, k, cols], w1l[par][:, k, cols],
                            x2h[:, bass.ds(b, 1), k, :].rearrange("p o n -> p (o n)"),
                            x2l[:, bass.ds(b, 1), k, :].rearrange("p o n -> p (o n)"))]).then_inc(f1_ready, 1)
                    pe.wait_ge(f2_free, 1 + 4 * it)
                    for f in range(4):
                        pe.wait_ge(g_hi, 1 + 4 * it + f + 1)
                        pe.wait_ge(g_lo, 1 + 4 * it + f + 1)
                        for i in range(NT):
                            rows = slice(i * P, (i + 1) * P)
                            terms = three(gh[:, f, rows], gl[:, f, rows], w2h[par][:, f, :], w2l[par][:, f, :])
                            for n, (a_, b_) in enumerate(terms):
                                last = pe.matmul(bank[4 + i], a_, b_, start=(f == 0 and n == 0),
                                                 stop=(f == 3 and n == 2))
                            if f == 3:
                                last.then_inc(f2_ready, 1)

            pe.wait_ge(f2_free, 1 + 4 * B * FB)
            pe.wait_ge(w_hi, 8 * (FB + 1))
            pe.wait_ge(w_lo, 8 * (FB + 1))
            with pe.Fori(0, B) as b:
                def keys_values(half, i):
                    rows = slice(i * P, (i + 1) * P)
                    cols = slice(half * D, (half + 1) * D)
                    product(bank[i], [m for k in range(KC) for m in three(
                        dth[:, k, rows], dtl[:, k, rows], wkvh[:, k, cols], wkvl[:, k, cols])]).then_inc(q_ready, 1)

                pe.wait_ge(dt_hi, b + 1)
                pe.wait_ge(dt_lo, 1 + b + 1)
                for i in range(NT):
                    pe.wait_ge(v_copied, 4 * b + i + 1)
                    keys_values(0, i)
                pe.wait_ge(ln_xn, 1 + NT * (2 * B + b + 1))
                for k in range(KF):
                    pe.wait_ge(q_free, 12 * b + k + 1)
                    transposes(bank[4 + k], lambda i: tok[:, i, k * P:(k + 1) * P]).then_inc(q_ready, 1)
                for i in range(NT):
                    pe.wait_ge(q_free, 4 + 12 * b + i + 1)
                    keys_values(1, i)
                pe.wait_ge(q_free, 4 + 12 * b + 8)
                for i in range(NT):
                    rows = slice(i * P, (i + 1) * P)
                    product(bank[4 + i], [m for k in range(KF) for m in three(
                        yth[:, k, rows], ytl[:, k, rows], wqh[:, k, :], wql[:, k, :])]).then_inc(q_ready, 1)

            def event(it, kind, q, n):
                def wait(sem_, first, per):
                    if it is not None:
                        pe.wait_ge(sem_, first + per * it)
                    elif first > 0:
                        pe.wait_ge(sem_, first)

                def v_bank():
                    if kind == "M" and q < 2:
                        if q or n >= 4:
                            wait(v_free, V_NUMBER["M", (16 * q + n - 4) // 16, (n - 4) % 16] + 1, V_PER)
                    else:
                        wait(v_free, V_NUMBER[kind, q, n] - 1, V_PER)
                    return v_place(kind, q, n)

                ring = q % RING
                if kind == "S":
                    pr, what = divmod(n, 2)
                    if n == 0:
                        wait(stg_done, q, C2_BODY)
                    if q:
                        wait(s_done, 4 * q + n, 4 * C2_BODY)
                    elif n == 0:
                        pe.wait_ge(first_done, 2)
                    transposes(s_bank(q, n), lambda i: stg[:, q % 2, what, i, 2 * pr:2 * pr + 2, :].rearrange(
                        "p h r -> p (h r)")).then_inc(s_ready, 1)
                elif kind == "M":
                    i, h = divmod(n, 4)
                    if n == 0:
                        wait(s_done, 4 * (q + 1), 4 * C2_BODY)
                    r = 64 * (h % 2)
                    pe.matmul(v_bank(), qst[r:r + 64, ring, h // 2, i * P:(i + 1) * P],
                              kst[r:r + 64, ring, h // 2, :], start=True, stop=True).then_inc(v_ready, 1)
                elif kind == "R":
                    wait(nm_lo, q + 1, C2_BODY)
                    transposes(v_bank(), lambda i: nms[:, i].rearrange("p h s -> p (h s)"), rows=8).then_inc(v_ready, 1)
                elif kind == "QK":
                    kt, pr = divmod(n, 2)
                    gi = 8 * q + n
                    if n == 0:
                        wait(mx_dma, 64 * (q + 1), 64 * C2_BODY)
                        if q == 0 and it is None:
                            pe.wait_ge(v_free, V_NUMBER["M", 1, 15] + 1)
                    wait(exp_done, gi - 1, 8 * C2_BODY)
                    for hp in range(2):
                        r = 64 * hp
                        last = pe.matmul(bank[2 * (gi % 2) + hp], kst[r:r + 64, ring, pr, kt * P:(kt + 1) * P],
                                         qst[r:r + 64, ring, pr, :], start=True, stop=True)
                    last.then_inc(lt_ready, 1)
                elif kind == "AV":
                    if n == 0:
                        wait(ot_done, q, C2_BODY)
                        wait(va_done, q + 1, C2_BODY)
                    wait(exp_done, 8 * q + 2 * n + 2, 8 * C2_BODY)
                    for h in range(4):
                        gi = 8 * q + 2 * n + h // 2
                        last = pe.matmul(bank[4][32 * h:32 * h + HD + 1, :], va[:, q % 2, n, h, :],
                                         wt[:, gi % 4, h % 2, :], start=(n == 0), stop=(n == NT - 1))
                    last.then_inc(av_done, 1)
                else:
                    wait(ot_done, q + 1, C2_BODY)
                    transposes(v_bank(), lambda i: ots[:, i * P:(i + 1) * P]).then_inc(v_ready, 1)

            def transpose_att(b):
                pe.wait_ge(at_copy, b + 1)
                for k in range(KF):
                    transposes(bank[k], lambda i: atok[:, i, k * P:(k + 1) * P]).then_inc(o_ready, 1)

            pe.wait_ge(q_free, 4 + 12 * B)
            pe.wait_ge(v_copied, 4 + 4 * B)
            pe.wait_ge(ot_init, 1)
            for s in C2_HEAD:
                for ev in attention_step(s):
                    event(None, *ev)
            with pe.Fori(0, C2_LOOPS) as it:
                for j in range(C2_BODY):
                    for ev in attention_step(1 + j):
                        event(it, *ev)
            for s in C2_TAIL:
                if s == C2_TAIL[3]:
                    pe.wait_ge(tn_sum, 1)
                    pe.wait_ge(s_done, 4 * NQ)
                    pe.wait_ge(ones_set, 1)
                    pe.matmul(bank[5][:, 0:2], ones, scl[:, 0:2], start=True, stop=True).then_inc(tn_all, 1)
                for ev in attention_step(s):
                    if ev == ("O", NQ - 1, 0):
                        pe.wait_ge(exp_done, 8 * NQ)
                        transpose_att(0)
                    event(None, *ev)

            pe.wait_ge(cw_hi, 2)
            pe.wait_ge(cw_lo, 1)

            def transpose_ln(b):
                pe.wait_ge(ln_xn, 1 + NT * (3 * B + b + 1))
                for k in range(KF):
                    transposes(bank[4 + k], lambda i: ftok[:, i, k * P:(k + 1) * P]).then_inc(o_ready, 1)

            def out_projection(freed):
                pe.wait_ge(o_free, freed)
                for i in range(NT):
                    rows = slice(i * P, (i + 1) * P)
                    product(bank[i], [m for k in range(KF) for m in three(
                        ath[:, k, rows], atl[:, k, rows], woh[:, k, :], wol[:, k, :])]).then_inc(o_ready, 1)

            def feed_forward(freed):
                pe.wait_ge(o_free, freed)
                for i in range(NT):
                    rows = slice(i * P, (i + 1) * P)
                    product(bank[4 + i], [m for k in range(KF) for m in (
                        (fth[:, k, rows], tern[:, k, :]), (ftl[:, k, rows], tern[:, k, :]))]).then_inc(o_ready, 1)

            out_projection(KF)
            pe.wait_ge(ot_done, NQ)
            pe.wait_ge(v_free, len(V_NUMBER))
            with pe.Fori(1, B) as b:
                n0 = o_first(b)
                pe.wait_ge(ln_agg, NT * (3 * B + b))
                transpose_att(b)
                pe.wait_ge(o_free, n0)
                transpose_ln(b - 1)
                out_projection(n0 + 4)
                feed_forward(n0 + 8)
            pe.wait_ge(o_free, 16 * B - 8)
            transpose_ln(B - 1)
            feed_forward(16 * B - 4)

        @block.scalar
        def _(act):
            def ln_apply(n, b, dst):
                act.wait_ge(ln_rstd, n + 1)
                for i in range(NT):
                    act.activation(dst[:, i, :], tile_of(b, i), ACT.Identity, scale=rstd[:, i:i + 1],
                                   bias=shift[:, i:i + 1]).then_inc(ln_xn, 1)

            act.wait_ge(ld_wqk, 32)
            act.activation(wqkh[:], wqk[:], ACT.Copy).then_inc(wqk_hi, 1)

            def split_ct(b):
                act.wait_ge(ld_ct, 16 * (b + 1))
                act.activation(cth[:], ct[:], ACT.Copy).then_inc(ct_hi, 1)

            def a_group(n0, n, b_):
                act.wait_ge(a_ready, n0 + n + 1)
                return bank[b_]

            def hi_qk(n0, n):
                for j, dst in enumerate((qh, kh)):
                    act.activation(dst[:], a_group(n0, n + j, E_BANK + j), ACT.Identity, bias=bqk[:, j:j + 1]).then_inc(a_hi, 1)

            def exps(b):
                for i in range(NT):
                    act.wait_ge(e_max, NT * b + i + 1)
                    act.activation(att[:, i, :], bank[E_BANK + i], ACT.Exp, bias=nmax[:, i:i + 1],
                                   accum_out=rsum[:, i:i + 1]).then_inc(e_exp, 1)

            def normalise(b):
                for i in range(NT):
                    act.wait_ge(e_rec, NT * b + i + 1)
                    act.activation(att[:, i, :], att[:, i, :], ACT.Copy, scale=small[:, 12 + i:13 + i]).then_inc(e_att, 1)

            def hi_x2(b, n0, n):
                hi_parts(lambda k: x2h[:, bass.ds(b, 1), k, :].rearrange("p o n -> p (o n)"), n0, n)

            def hi_parts(dst, n0, n):
                for k in range(KF):
                    act.activation(dst(k), a_group(n0, n + k, k), ACT.Copy).then_inc(a_hi, 1)

            def router_exp(b):
                act.wait_ge(rt_z, NT * (b + 1))
                act.activation(small[:, NT:2 * NT], small[:, 0:NT], ACT.Exp, scale=-1.0,
                               bias=minus_rb[:, 0:1]).then_inc(rt_exp, 1)

            split_ct(0)
            act.wait_ge(ld_const, 16 * N_CONST)
            hi_qk(0, 0)
            ln_apply(0, 0, xn1)
            split_ct(1)
            exps(0)
            hi_parts(lambda k: xth[:, k, :], 0, 2)
            normalise(0)
            hi_parts(lambda k: atth[:, k, :], 0, 6)
            hi_qk(0, 10)
            ln_apply(1, 1, xn1)

            def a_iteration(j, more):
                n0 = a_first(j)
                if more:
                    split_ct(j + 2)
                exps(j + 1)
                normalise(j + 1)
                hi_parts(lambda k: xth[:, k, :], n0, 4)
                ln_apply(2 * j + 2, j, xn2)
                hi_parts(lambda k: atth[:, k, :], n0, 8)
                if more:
                    hi_qk(n0, 12)
                hi_x2(j, n0, 14 if more else 12)
                router_exp(j)
                if more:
                    ln_apply(2 * j + 3, j + 2, xn1)

            with act.Fori(0, B - 2) as j:
                a_iteration(j, True)
            a_iteration(B - 2, False)
            ln_apply(2 * B - 1, B - 1, xn2)
            hi_x2(B - 1, A_TAIL, 4)
            router_exp(B - 1)
            act.wait_ge(tab, 8)
            for n, dst in ((0, cosd), (1, sind)):
                a_ = ang[:, n].rearrange("p t a f -> p t (a f)")
                act.activation(dst[:, :, :, 0], a_, ACT.Sin, scale=1.0 if n == 0 else -1.0).then_inc(tab_sin, 1)
                act.activation(dst[:, :, :, 1], a_, ACT.Sin).then_inc(tab_sin, 1)

            act.wait_ge(a_free, A_ALL)
            for fb in range(FB):
                with act.Fori(0, B) as b:
                    it = b + fb * B
                    act.wait_ge(g_lo, 1 + 4 * it)
                    act.wait_ge(g_hi, 1 + 4 * it)
                    for f in range(4):
                        act.wait_ge(f1_ready, 4 * it + f + 1)
                        act.activation(g[:, f, :], bank[f], ACT.Gelu_apprx_tanh,
                                       bias=b1[:, 4 * fb + f:4 * fb + f + 1]).then_inc(f1_gelu, 1)

            def split_dt(b):
                act.wait_ge(dt_ld, 16 * (b + 1))
                act.activation(dth[:], dt_[:], ACT.Copy).then_inc(dt_hi, 1)

            def c1_batch(b, more):
                for k in range(KF):
                    act.wait_ge(q_ready, 1 + 16 * b + 4 + k + 1)
                    act.activation(yth[:, k, :], bank[4 + k], ACT.Copy).then_inc(q_hi, 1)
                for i in range(NT):
                    act.wait_ge(q_ready, 1 + 16 * b + 8 + i + 1)
                    act.activation(vr[:, bass.ds(QUADS * b, QUADS), i, :],
                                   bank[i].rearrange("p (q n) -> p q n", q=QUADS), ACT.Copy).then_inc(v_copied, 1)
                if more:
                    split_dt(b + 1)
                    ln_apply(2 * B + 1 + b, b + 1, tok)

            act.wait_ge(f1_ready, 4 * B * FB)
            split_dt(0)
            act.wait_ge(f2_free, 1 + 4 * B * FB)
            ln_apply(2 * B, 0, tok)
            with act.Fori(0, B - 1) as b:
                c1_batch(b, True)
            c1_batch(B - 1, False)

            def event(it, kind, q, n):
                def wait(sem_, first, per):
                    if it is not None:
                        act.wait_ge(sem_, first + per * it)
                    elif first > 0:
                        act.wait_ge(sem_, first)

                if kind == "S":
                    pr, what = divmod(n, 2)
                    wait(lt_ready, 8 * (q - RING + 1), 8 * C2_BODY)
                    wait(s_ready, 4 * q + n + 1, 4 * C2_BODY)
                    act.activation((qst, kst)[what][:, q % RING, pr, :], s_bank(q, n), ACT.Copy).then_inc(s_done, 1)
                elif kind == "QK":
                    gi = 8 * q + n
                    wait(lt_ready, gi + 1, 8 * C2_BODY)
                    wait(av_done, (gi - 4) // 2 + 1, 4 * C2_BODY)
                    two = 2 * (gi % 2)
                    act.activation(wt[:, gi % 4, :, :], banks[:, two:two + 2, :], ACT.Exp,
                                   scale=float(HD) ** -0.5).then_inc(exp_done, 1)
                elif kind == "AV" and n == NT - 1:
                    wait(av_done, 4 * (q + 1), 4 * C2_BODY)
                    if q > 0:
                        wait(v_ready, V_NUMBER["O", q - 1, 0] + 1, V_PER)
                    elif it is not None:
                        wait(v_ready, V_NUMBER["O", q - 1 + C2_BODY, 0] + 1 - V_PER, V_PER)
                    act.activation(ots[:], bank[4], ACT.Copy).then_inc(ot_done, 1)

            act.wait_ge(q_free, 4 + 12 * B)
            for s in C2_HEAD:
                for ev in attention_step(s):
                    event(None, *ev)
            with act.Fori(0, C2_LOOPS) as it:
                for j in range(C2_BODY):
                    for ev in attention_step(1 + j):
                        event(it, *ev)
            def copy_att(b):
                act.activation(atok[:].rearrange("p i (q n) -> p i q n", q=QUADS),
                               qr[:, bass.ds(QUADS * b, QUADS), :, :].rearrange("p q i n -> p i q n"),
                               ACT.Copy).then_inc(at_copy, 1)

            def hi_o(dst, n0, first_bank):
                for k in range(KF):
                    act.wait_ge(o_ready, n0 + k + 1)
                    act.activation(dst[:, k, :], bank[first_bank + k], ACT.Copy).then_inc(o_hi, 1)

            for s in C2_TAIL:
                if s == C2_TAIL[-1]:
                    act.wait_ge(s_ready, 4 * NQ)
                    copy_att(0)
                for ev in attention_step(s):
                    event(None, *ev)

            hi_o(ath, 0, 0)
            act.wait_ge(v_free, len(V_NUMBER))
            copy_att(1)
            ln_apply(3 * B, 0, ftok)
            with act.Fori(1, B - 1) as b:
                hi_o(ath, o_first(b), 0)
                hi_o(fth, o_first(b) + 4, 4)
                copy_att(b + 1)
                ln_apply(3 * B + b, b, ftok)
            hi_o(ath, o_first(B - 1), 0)
            hi_o(fth, o_first(B - 1) + 4, 4)
            ln_apply(4 * B - 1, B - 1, ftok)
            hi_o(fth, 16 * B - 8, 4)

        @block.vector
        def _(dve):
            def ln_aggregate(n, slot=0):
                for i in range(NT):
                    if isinstance(n, int):
                        if n and i == 0:
                            dve.wait_ge(ln_rstd, n)
                        dve.wait_ge(ln_stats, NT * n + i + 1)
                    else:
                        if i == 0:
                            wait_apart(dve, ln_rstd, n)
                        wait_apart(dve, ln_stats, NT * n + i + 1)
                    dve.bn_aggr(mv[:, i, :], stats[:, slot, i, :]).then_inc(ln_agg, 1)

            def ln_tiles(b, slot):
                for i in range(NT):
                    dve.bn_stats(stats[:, slot, i, :], tile_of(b, i)).then_inc(ln_stats, 1)

            def ln_statistics(n, b, slot=0):
                ln_tiles(b, slot)
                ln_aggregate(n, slot)

            def low_parts(dst, dst_hi, h0, h):
                for k in range(KF):
                    dve.wait_ge(a_hi, h0 + h + k + 1)
                    dve.tensor_tensor(dst(k), bank[k], f32(dst_hi(k)), ALU.subtract).then_inc(a_free, 1)

            def low_qk(h0, h):
                for j, (dst, dst_hi) in enumerate(((ql, qh), (kl, kh))):
                    dve.wait_ge(a_hi, h0 + h + j + 1)
                    dve.scalar_tensor_tensor(dst[:], bank[E_BANK + j], bqk[:, j:j + 1], f32(dst_hi[:]),
                                             ALU.add, ALU.subtract).then_inc(a_free, 1)

            def maxima(b):
                for i in range(NT):
                    dve.wait_ge(e_ready, NT * b + i + 1)
                    dve.tensor_reduce(nmax[:, i:i + 1], bank[E_BANK + i], AX.X, ALU.max, negate=True).then_inc(e_max, 1)

            def reciprocals(b):
                for i in range(NT):
                    dve.wait_ge(e_exp, NT * b + i + 1)
                    dve.reciprocal(small[:, 12 + i:13 + i], rsum[:, i:i + 1]).then_inc(e_rec, 1)

            def add_att(b, n0, tiles):
                for i in tiles:
                    dve.wait_ge(a_ready, n0 + i + 1)
                    dve.tensor_tensor(tile_of(b, i), xm_bank(i), tile_of(b, i), ALU.add).then_inc(a_free, 1)

            def new_statistics(b, n0, tiles):
                for i in tiles:
                    if isinstance(b, int):
                        dve.wait_ge(a_free, n0 + i + 1)
                    else:
                        wait_apart(dve, a_free, n0 + i + 1)
                    dve.bn_stats(stats[:, 0, i, :], tile_of(b, i)).then_inc(ln_stats, 1)

            def router_scores(b, n):
                dve.wait_ge(ln_xn, 1 + NT * (n + 1))
                for i in range(NT):
                    if i:
                        dve.wait_ge(rt_z, NT * b + i)
                    dve.tensor_tensor_reduce(scratch[:], xn2[:, i, :], rw[:], 1.0, 0.0, ALU.mult, ALU.add,
                                             small[:, i:i + 1]).then_inc(rt_z, 1)

            def router_weight(b):
                dve.wait_ge(rt_exp, b + 1)
                dve.tensor_scalar(small[:, 2 * NT:3 * NT], small[:, NT:2 * NT], 1.0, None, ALU.add).then_inc(rt_den, 1)
                dve.wait_ge(rt_den, b + 1)
                dve.reciprocal(router[:, bass.ds(NT * b, NT)], small[:, 2 * NT:3 * NT])
                dve.reciprocal(small[:, 4 * NT:5 * NT], small[:, 2 * NT:3 * NT]).then_inc(rt_w, 1)

            def add_b2(b):
                dve.wait_ge(rt_w, b + 1)
                for i in range(NT):
                    dve.wait_ge(x_res, NT * b + i + 1)
                    dve.scalar_tensor_tensor(tile_of(b, i), b2[:], router[:, bass.ds(NT * b + i, 1)], tile_of(b, i),
                                             ALU.mult, ALU.add).then_inc(x_b2, 1)

            dve.wait_ge(ld_x, 16)
            ln_statistics(0, 0)
            dve.wait_ge(ld_const, 16 * N_CONST)
            dve.tensor_scalar(minus_rb[:], rb[:], -1.0, None, ALU.mult)
            two_pi = 2 * np.pi
            c1 = 6.28125
            c2 = float(np.round((two_pi - c1) * 2.0 ** 20)) / 2.0 ** 20
            c3 = two_pi - c1 - c2
            magic = 1.5 * 2.0 ** 23
            freqs = (np.float32(ROPE_BASE) ** (-np.arange(HALF, dtype=np.float32) / np.float32(HALF))).astype(np.float32)
            for f in range(HALF):
                last_ = dve.tensor_scalar(ang[:, 1, :, :, f], pos[:], float(freqs[f]), None, ALU.mult)
            last_.then_inc(tab, 1)
            dve.wait_ge(tab, 1)
            dve.tensor_scalar(ang[:, 0], ang[:, 1], float(np.pi / 2), None, ALU.add).then_inc(tab, 1)
            dve.wait_ge(tab, 2)
            both = ang[:, 0:2].rearrange("p n t a f -> p (n t a f)")
            dve.tensor_scalar(turns[:], both, 1.0 / two_pi, magic, ALU.mult, ALU.add).then_inc(tab, 1)
            dve.wait_ge(tab, 3)
            dve.tensor_scalar(turns[:], turns[:], magic, None, ALU.subtract).then_inc(tab, 1)
            for n, c in enumerate((c1, c2, c3)):
                dve.wait_ge(tab, 4 + n)
                dve.scalar_tensor_tensor(both, turns[:], -c, both, ALU.mult, ALU.add).then_inc(tab, 1)
            dve.wait_ge(tab, 7)
            dve.tensor_scalar(both, both, 3.1415925, -3.1415925, ALU.min, ALU.max).then_inc(tab, 1)

            def split_hi(fb, c):
                dve.wait_ge(w_ld, 32 * (4 * fb + c + 1))
                for j, dst in enumerate((w1h, w2h)):
                    dve.tensor_copy(dst[fb % 2][:, bass.ds(c, 1), :], wst[:, bass.ds(c, 1), j, :]).then_inc(w_hi, 1)

            low_qk(0, 0)
            maxima(0)
            reciprocals(0)
            low_parts(lambda k: xtl[:, k, :], lambda k: xth[:, k, :], 0, 2)
            low_parts(lambda k: attl[:, k, :], lambda k: atth[:, k, :], 0, 6)
            dve.wait_ge(ld_x, 32)
            ln_statistics(1, 1, 1)
            low_qk(0, 10)

            def a_iteration(j, more):
                n0, h0 = a_first(j), hi_first(j)
                add_att(j, n0, (0, 1))
                maxima(j + 1)
                reciprocals(j + 1)
                new_statistics(j, n0, (0, 1))
                for i in (2, 3):
                    add_att(j, n0, (i,))
                    new_statistics(j, n0, (i,))
                ln_aggregate(2 * j + 2)
                low_parts(lambda k: xtl[:, k, :], lambda k: xth[:, k, :], h0, 0)
                if more:
                    wait_apart(dve, ld_x, 16 * (j + 3))
                    ln_tiles(j + 2, 1)
                low_parts(lambda k: attl[:, k, :], lambda k: atth[:, k, :], h0, 4)
                if more:
                    ln_aggregate(2 * j + 3, 1)
                    low_qk(h0, 8)
                h = 10 if more else 8
                x2_j = lambda m: (lambda k: m[:, bass.ds(j, 1), k, :].rearrange("p o n -> p (o n)"))
                router_scores(j, 2 * j + 2)
                low_parts(x2_j(x2l), x2_j(x2h), h0, h)
                router_weight(j)

            with dve.Fori(0, B - 2) as j:
                a_iteration(j, True)
            a_iteration(B - 2, False)
            last = B - 1
            for i in range(NT):
                add_att(last, A_TAIL, (i,))
                new_statistics(last, A_TAIL, (i,))
                if i < NT - 1:
                    split_hi(0, i)
            ln_aggregate(2 * B - 1)
            split_hi(0, NT - 1)
            add_b2(B - 2)
            router_scores(last, 2 * B - 1)
            low_parts(lambda k: x2l[:, last, k, :], lambda k: x2h[:, last, k, :], HI_TAIL, 0)
            router_weight(last)
            add_b2(last)

            for fb in range(FB):
                with dve.Fori(0, B) as b:
                    it = b + fb * B
                    for f in range(4):
                        dve.wait_ge(f1_gelu, 1 + 4 * it + f + 1)
                        dve.tensor_copy(gh[:, f, :], g[:, f, :]).then_inc(g_hi, 1)
                    if fb:
                        dve.wait_ge(f2_ready, 4 * B * fb)
                    else:
                        dve.wait_ge(x_b2, NT * B)
                        dve.wait_ge(tab_sin, 4)
                    split_hi(fb + 1, b)
                    for i in range(NT):
                        dve.wait_ge(f2_ready, 4 * it + i + 1)
                        dve.scalar_tensor_tensor(tile_of(b, i), bank[4 + i], router[:, bass.ds(NT * b + i, 1)],
                                                 tile_of(b, i), ALU.mult, ALU.add).then_inc(f2_free, 1)

            dve.wait_ge(f2_free, 1 + 4 * B * FB)
            dve.wait_ge(w_lo, 8 * (FB + 1))
            ln_statistics(2 * B, 0)

            def rotate(b, c0, bank0, dst, slot0):
                for i in range(NT):
                    n = slot0 + i
                    dve.wait_ge(q_ready, 1 + 16 * b + c0 + i + 1)
                    dve.wait_ge(rope_done, 1 + 2 * NT * b + max(0, n - 1))
                    z = bank[bank0 + i]
                    cos_i, sin_i = (tb[:, bass.ds(NT * b + i, 1), :, :] for tb in (cosd, sind))
                    dve.tensor_tensor(dst[:, bass.ds(QUADS * b, QUADS), i, :].rearrange("p q (h f) -> p q h f", h=4),
                                      z.rearrange("p (q h f) -> p q h f", q=QUADS, h=4),
                                      cos_i.rearrange("p o f e -> p o (f e)").unsqueeze(1).to_broadcast([P, QUADS, 4, HD]),
                                      ALU.mult)
                    z2 = z.rearrange("p (h f e) -> p h f e", h=H, e=2)
                    r2 = rbuf[:, n % 2, :].rearrange("p (h f e) -> p h f e", h=H, e=2)
                    for e in range(2):
                        last = dve.tensor_tensor(r2[:, :, :, e], z2[:, :, :, 1 - e],
                                                 sin_i[:, :, :, e].to_broadcast([P, H, 2 * HALF]), ALU.mult)
                    last.then_inc(q_free, 1)

            def c1_batch(b, more):
                rotate(b, 0, 0, kr, 0)
                for k in range(KF):
                    dve.wait_ge(q_hi, KF * b + k + 1)
                    dve.tensor_tensor(ytl[:, k, :], bank[4 + k], f32(yth[:, k, :]), ALU.subtract).then_inc(q_free, 1)
                if more:
                    ln_statistics(2 * B + 1 + b, b + 1)
                    dve.wait_ge(dt_lo, 1 + b + 2)
                rotate(b, 12, 4, qr, NT)

            with dve.Fori(0, B - 1) as b:
                c1_batch(b, True)
            c1_batch(B - 1, False)

            dve.wait_ge(q_ready, 1 + 16 * B)
            dve.wait_ge(v_copied, 4 + 4 * B)
            dve.memset(ones, 1.0).then_inc(ones_set, 1)
            dve.memset(va[:].rearrange("p r i h d -> p (r i h d)"), 1.0).then_inc(stg_zero, 1)
            for par in range(2):
                dve.memset(stg[:, par, 0, :, :, ROW_MAX:64], 0.0)
                dve.memset(stg[:, par, 1, :, :, ROW_MAX:ROW_MAX + 2], 1.0)
                last = dve.memset(stg[:, par, 1, :, :, ROW_MAX + 2:64], 0.0)
            last.then_inc(stg_zero, 1)
            dve.wait_ge(rope_done, 1 + 2 * NT)
            for what, src, lo_at, hi_at in STACKS:
                sv = stg[:, 0, what].rearrange("p i h (j d) -> p i h j d", j=4)
                src_q = src[:, 0, :, :].rearrange("p i (h d) -> p i h d", h=4)
                dve.tensor_copy(r32(sv[:, :, :, 0, :]), src_q).then_inc(first_hi, 1)
                dve.wait_ge(first_hi, what + 1)
                dve.tensor_copy(sv[:, :, :, hi_at, :], sv[:, :, :, 0, :])
                dve.tensor_tensor(sv[:, :, :, lo_at, :], src_q, sv[:, :, :, 0, :], ALU.subtract).then_inc(first_done, 1)
            dve.memset(bank[4], 0.0).then_inc(ot_init, 1)

            def wait_step(it, sem_, first, per):
                if it is not None:
                    dve.wait_ge(sem_, first + per * it)
                elif first > 0:
                    dve.wait_ge(sem_, first)

            def max_hi(it, q):
                wait_step(it, v_free, V_NUMBER["M", q, 15] + 1, V_PER)
                dve.tensor_copy(r32(nms[:, :, :, 0]), nmx[:, q % 2]).then_inc(nm_hi, 1)

            def max_lo(it, q):
                wait_step(it, nm_hi, q + 1, C2_BODY)
                dve.tensor_tensor(nms[:, :, :, 1], nmx[:, q % 2], nms[:, :, :, 0], ALU.subtract).then_inc(nm_lo, 1)

            def event(it, kind, q, n):
                def wait(sem_, first, per):
                    wait_step(it, sem_, first, per)

                if kind not in ("M", "R", "O"):
                    return
                number = V_NUMBER[kind, q, n]
                wait(v_ready, number + 1, V_PER)
                src = v_place(kind, q, n)
                if kind == "M":
                    i, h = divmod(n, 4)
                    dve.tensor_reduce(nmx[:, q % 2, i, h:h + 1], src, AX.X, ALU.max, negate=True).then_inc(v_free, 1)
                    if n == 0 and q > 0:
                        max_hi(it, q - 1)
                    if n == 1 and q > 0:
                        max_lo(it, q - 1)
                    if n == 15 and q == NQ - 1:
                        max_hi(it, q)
                        max_lo(it, q)
                elif kind == "R":
                    dve.tensor_copy(mrow[:, q % 2, :], src[0:8, :]).then_inc(v_free, 1)
                else:
                    o = src.rearrange("p (i h r) -> p i h r", i=NT, h=4)
                    dve.reciprocal(rinv[:, q % 2], o[:, :, :, HD]).then_inc(o_rinv, 1)
                    wait(o_rinv, q + 1, C2_BODY)
                    dst = qr[:, q, :, :] if it is None else qr[:, bass.ds(q + C2_BODY * it, 1), :, :].rearrange(
                        "p o i n -> p (o i) n")
                    dve.tensor_tensor(dst.rearrange("p i (h d) -> p i h d", h=4), o[:, :, :, 0:HD],
                                      rinv[:, q % 2].unsqueeze(3).to_broadcast([P, NT, 4, HD]), ALU.mult).then_inc(v_free, 1)

            for s in C2_HEAD:
                for ev in attention_step(s):
                    event(None, *ev)
            with dve.Fori(0, C2_LOOPS) as it:
                for j in range(C2_BODY):
                    for ev in attention_step(1 + j):
                        event(it, *ev)
            def low_o(dst, dst_hi, h, first_bank):
                for k in range(KF):
                    dve.wait_ge(o_hi, h + k + 1)
                    dve.tensor_tensor(dst[:, k, :], bank[first_bank + k], f32(dst_hi[:, k, :]), ALU.subtract).then_inc(o_free, 1)

            wlin = wraw[:].rearrange("p k n -> p (k n)")
            tlin = tern[:].rearrange("p k n -> p (k n)")
            for s in C2_TAIL:
                if s == C2_TAIL[2]:
                    dve.wait_ge(cw_ld, 32)
                    dve.memset(scl[:, 1:2], 0.0)
                    dve.tensor_reduce(scl[:, 0:1], wlin, AX.X, ALU.add, apply_absolute_value=True).then_inc(tn_sum, 1)
                if s == C2_TAIL[3]:
                    dve.wait_ge(tn_all, 1)
                    dve.tensor_scalar(scl[:, 2:3], bank[5][:, 0:1], 1.0 / (D * D), TERNARY_EPS, ALU.mult, ALU.add)
                    dve.tensor_scalar(scl[:, 3:4], bank[5][:, 0:1], -1.0 / (D * D), None, ALU.mult).then_inc(tn_scale, 1)
                    dve.wait_ge(tn_scale, 1)
                    dve.tensor_scalar(scl[:, 0:1], scl[:, 2:3], 0.5, None, ALU.mult)
                    dve.tensor_scalar(scl[:, 1:2], scl[:, 2:3], -0.5, None, ALU.mult).then_inc(tn_done, 1)
                    dve.wait_ge(tn_done, 1)
                    dve.tensor_scalar(tlin, wlin, scl[:, 0:1], None, ALU.is_gt).then_inc(tn_done, 1)
                    dve.wait_ge(tn_done, 2)
                    dve.scalar_tensor_tensor(tlin, wlin, scl[:, 1:2], f32(tlin), ALU.is_lt, ALU.subtract).then_inc(cw_hi, 1)
                for ev in attention_step(s):
                    if ev == ("O", NQ - 1, 0):
                        low_o(atl, ath, 0, 0)
                    event(None, *ev)
                    if ev == ("R", NQ - 1, 0):
                        dve.wait_ge(cw_ld, 16)
                        dve.tensor_copy(woh[:].rearrange("p k n -> p (k n)"), wlin).then_inc(cw_hi, 1)

            def add_out(b, n):
                for i in range(NT):
                    dve.wait_ge(bo_done, NT * b + i + 1)
                    dve.wait_ge(o_ready, n + i + 1)
                    dve.tensor_tensor(tile_of(b, i), bank[i], tile_of(b, i), ALU.add).then_inc(o_free, 1)
                    if isinstance(b, int):
                        dve.wait_ge(o_free, n + i + 1)
                    else:
                        wait_apart(dve, o_free, n + i + 1)
                    dve.bn_stats(stats[:, 0, i, :], tile_of(b, i)).then_inc(ln_stats, 1)
                ln_aggregate(3 * B + b)

            def add_ff(b, n):
                for i in range(NT):
                    dve.wait_ge(x_bias, NT * b + i + 1)
                    dve.wait_ge(o_ready, n + i + 1)
                    dve.scalar_tensor_tensor(tile_of(b, i), bank[4 + i], scl[:, 3:4], tile_of(b, i),
                                             ALU.mult, ALU.add).then_inc(o_free, 1)

            add_out(0, 4)
            with dve.Fori(1, B) as b:
                n0 = o_first(b)
                low_o(atl, ath, 8 * b - 4, 0)
                low_o(ftl, fth, 8 * b, 4)
                add_out(b, n0 + 8)
                add_ff(b - 1, n0 + 12)
            low_o(ftl, fth, 8 * B - 4, 4)
            add_ff(B - 1, 16 * B - 4)

        @block.gpsimd
        def _(pool):
            def rstd_of(n):
                if isinstance(n, int):
                    pool.wait_ge(ln_agg, NT * (n + 1))
                    pool.wait_ge(ln_xn, 1 + NT * n)
                else:
                    wait_apart(pool, ln_agg, NT * (n + 1))
                    wait_apart(pool, ln_xn, 1 + NT * n)
                pool.tensor_scalar(shift[:], mv[:, :, 0], -1.0, 0.0, ALU.mult, ALU.add)
                pool.tensor_scalar(rstd[:], mv[:, :, 1], LN_EPS, 1.0, ALU.add, ALU.mult).then_inc(ln_eps, 1)
                pool.wait_ge(ln_eps, n + 1)
                pool.tensor_tensor(rstd[:], rstd[:], minus_half[:], ALU.pow).then_inc(ln_pow, 1)
                pool.wait_ge(ln_pow, n + 1)
                pool.tensor_tensor(shift[:], shift[:], rstd[:], ALU.mult).then_inc(ln_rstd, 1)

            pool.wait_ge(wqk_hi, 1)
            pool.tensor_tensor(wqkl[:], wqk[:], f32(wqkh[:]), ALU.subtract).then_inc(wqk_lo, 1)

            def split_ct(b):
                pool.wait_ge(ct_hi, b + 1)
                pool.tensor_tensor(ctl[:], ct[:], f32(cth[:]), ALU.subtract).then_inc(ct_lo, 1)

            def residual(b, n):
                for i in range(NT):
                    if isinstance(b, int):
                        pool.wait_ge(ln_xn, 1 + NT * n + i + 1)
                    else:
                        wait_apart(pool, ln_xn, 1 + NT * n + i + 1)
                    pool.tensor_tensor(tile_of(b, i), tile_of(b, i), xn2[:, i, :], ALU.add).then_inc(x_res, 1)

            def add_b2(b):
                for i in range(NT):
                    if i == 0:
                        wait_apart(pool, rt_w, b + 1)
                    if isinstance(b, int):
                        pool.wait_ge(x_res, NT * b + i + 1)
                    else:
                        wait_apart(pool, x_res, NT * b + i + 1)
                    pool.tensor_scalar(b2w[:, i % 2, :], b2[:], small[:, 4 * NT + i:4 * NT + i + 1], 0.0,
                                       ALU.mult, ALU.add).then_inc(b2_w, 1)
                    if isinstance(b, int):
                        pool.wait_ge(b2_w, NT * b + i + 1)
                    else:
                        wait_apart(pool, b2_w, NT * b + i + 1)
                    pool.tensor_tensor(tile_of(b, i), tile_of(b, i), b2w[:, i % 2, :], ALU.add).then_inc(x_b2, 1)

            split_ct(0)
            pool.wait_ge(ld_const, 16 * N_CONST)
            rstd_of(0)
            split_ct(1)
            rstd_of(1)

            def a_iteration(j, more):
                if more:
                    split_ct(j + 2)
                rstd_of(2 * j + 2)
                if more:
                    rstd_of(2 * j + 3)
                residual(j, 2 * j + 2)
                if more:
                    add_b2(j)

            with pool.Fori(0, B - 2) as j:
                a_iteration(j, True)
            a_iteration(B - 2, False)


            def split_lo(fb, c):
                if isinstance(c, int):
                    pool.wait_ge(w_hi, 2 * (4 * fb + c + 1))
                else:
                    wait_apart(pool, w_hi, 2 * (4 * fb + c + 1))
                for j, (dst, hi_) in enumerate(((w1l, w1h), (w2l, w2h))):
                    pool.tensor_tensor(dst[fb % 2][:, bass.ds(c, 1), :], wst[:, bass.ds(c, 1), j, :],
                                       f32(hi_[fb % 2][:, bass.ds(c, 1), :]), ALU.subtract).then_inc(w_lo, 1)

            for c in range(4):
                if c == 2:
                    rstd_of(2 * B - 1)
                split_lo(0, c)
            residual(B - 1, 2 * B - 1)
            for fb in range(FB):
                with pool.Fori(0, B) as b:
                    it = b + fb * B
                    for f in range(4):
                        pool.wait_ge(g_hi, 1 + 4 * it + f + 1)
                        pool.tensor_tensor(gl[:, f, :], g[:, f, :], f32(gh[:, f, :]), ALU.subtract).then_inc(g_lo, 1)
                    split_lo(fb + 1, b)


            def add_rotated(b, c0, dst, slot0):
                for i in range(NT):
                    n = slot0 + i
                    d = dst[:, bass.ds(QUADS * b, QUADS), i, :]
                    if isinstance(b, int):
                        pool.wait_ge(q_free, 4 + 12 * b + c0 + i + 1)
                    else:
                        wait_apart(pool, q_free, 4 + 12 * b + c0 + i + 1)
                    pool.tensor_tensor(d, d, rbuf[:, n % 2, :].rearrange("p (q n) -> p q n", q=QUADS),
                                       ALU.add).then_inc(rope_done, 1)

            def split_dt(b):
                pool.wait_ge(dt_hi, b + 1)
                pool.tensor_tensor(dtl[:], dt_[:], f32(dth[:]), ALU.subtract).then_inc(dt_lo, 1)

            def c1_batch(b, more):
                add_rotated(b, 0, kr, 0)
                if more:
                    rstd_of(2 * B + 1 + b)
                    split_dt(b + 1)
                add_rotated(b, 8, qr, NT)

            split_dt(0)
            pool.wait_ge(f2_free, 1 + 4 * B * FB)
            rstd_of(2 * B)
            with pool.Fori(0, B - 1) as b:
                c1_batch(b, True)
            c1_batch(B - 1, False)

            pool.wait_ge(q_ready, 1 + 16 * B)
            pool.wait_ge(q_free, 4 + 12 * B)
            pool.wait_ge(v_copied, 4 + 4 * B)
            pool.wait_ge(rope_done, 1 + 2 * NT * B)
            def stage(it, q):
                def wait(sem_, first, per):
                    if it is not None:
                        wait_apart(pool, sem_, first + per * it)
                    elif first > 0:
                        pool.wait_ge(sem_, first)

                def quad(m):
                    return m[:, q, :, :] if it is None else m[:, bass.ds(q + C2_BODY * it, 1), :, :].rearrange(
                        "p o i n -> p (o i) n")

                wait(s_ready, 4 * (q - 1), 4 * C2_BODY)
                for what, src, lo_at, hi_at in STACKS:
                    sv = stg[:, q % 2, what].rearrange("p i h (j d) -> p i h j d", j=4)
                    src_q = quad(src).rearrange("p i (h d) -> p i h d", h=4)
                    pool.tensor_copy(r32(sv[:, :, :, 0, :]), src_q).then_inc(stg_hi, 1)
                    wait(stg_hi, 2 * (q - 1) + what + 1, 2 * C2_BODY)
                    pool.tensor_copy(sv[:, :, :, hi_at, :], sv[:, :, :, 0, :])
                    last = pool.tensor_tensor(sv[:, :, :, lo_at, :], src_q, sv[:, :, :, 0, :], ALU.subtract)
                last.then_inc(stg_done, 1)

            def values(it, q):
                if it is not None:
                    wait_apart(pool, av_done, 4 * (q - 1) + 4 * C2_BODY * it)
                elif q >= 2:
                    pool.wait_ge(av_done, 4 * (q - 1))
                src = vr[:, q, :, :] if it is None else vr[:, bass.ds(q + C2_BODY * it, 1), :, :].rearrange(
                    "p o i n -> p (o i) n")
                pool.tensor_copy(va[:, q % 2, :, :, 0:HD], src.rearrange("p i (h d) -> p i h d", h=4)).then_inc(va_done, 1)

            pool.wait_ge(stg_zero, 2)
            for q in range(4):
                if q:
                    stage(None, q)
                if q < 2:
                    values(None, q)
            with pool.Fori(0, C2_LOOPS) as it:
                for j in range(C2_BODY):
                    stage(it, 4 + j)
                    values(it, 2 + j)
            values(None, NQ - 2)
            pool.wait_ge(cw_hi, 1)
            pool.tensor_tensor(wol[:].rearrange("p k n -> p (k n)"), wraw[:].rearrange("p k n -> p (k n)"),
                               f32(woh[:].rearrange("p k n -> p (k n)")), ALU.subtract).then_inc(cw_lo, 1)
            values(None, NQ - 1)

            def add_bout(b):
                for i in range(NT):
                    pool.tensor_tensor(tile_of(b, i), tile_of(b, i), boutb[:], ALU.add).then_inc(bo_done, 1)

            def add_bias(b):
                for i in range(NT):
                    if isinstance(b, int):
                        pool.wait_ge(ln_xn, 1 + NT * (3 * B + b) + i + 1)
                    else:
                        wait_apart(pool, ln_xn, 1 + NT * (3 * B + b) + i + 1)
                    pool.tensor_tensor(tile_of(b, i), tile_of(b, i), biasb[:], ALU.add).then_inc(x_bias, 1)

            pool.wait_ge(ld_cb, 32)
            add_bout(0)
            rstd_of(3 * B)
            with pool.Fori(1, B) as b:
                add_bout(b)
                add_bias(b - 1)
                rstd_of(3 * B + b)
            add_bias(B - 1)


def layouts(np_, v):
    c = np_.ascontiguousarray

    def over(a):
        return c(np_.broadcast_to(a.reshape(1, -1), (P, a.size)))

    return {
        "x": c(v["x"]),
        "ctx": c(v["ctx_1024"].transpose(0, 2, 1)),
        "pos": c(v["fside_BxSx2_0"].reshape(B * NT, P, 2).transpose(1, 0, 2)),
        "l0_wq": c(v["L0_xattn_Wq"].T),
        "l0_wk": c(v["L0_xattn_Wk"].T),
        "bqk": c(np_.stack([v["L0_xattn_bq"], v["L0_xattn_bk"]], axis=1)),
        "rw": over(v["L0_ffn_router_weight"]),
        "rb": over(v["L0_ffn_router_bias"]),
        "w1": c(v["L0_ffn_w1"]),
        "b1": c(v["L0_ffn_b1"].reshape(DFF // P, P).T),
        "w2": c(v["L0_ffn_w2"]),
        "b2": over(v["L0_ffn_b2"]),
        "l1_wq": c(v["L1_xattn_Wq"]),
        "l1_wkv": c(v["L1_xattn_Wkv"]),
        "l1_wout": c(v["L1_xattn_Wout"]),
        "bout": over(v["L1_xattn_bout"]),
        "l1_wt": c(v["L1_ffn_weight"].T),
        "bias": over(v["L1_ffn_bias"]),
        "ident": np_.eye(P, dtype=np_.float32),
        "minus_half": np_.full((P, NT), -0.5, np_.float32),
    }


def kernel(**inputs):
    import concourse.bacc as bacc
    from concourse.bass_utils import run_bass_kernel_spmd

    arrays = layouts(np, {k: np.asarray(v) for k, v in inputs.items()})
    nc = bacc.Bacc("TRN2", target_bir_lowering=False, num_devices=1)
    t = {k: nc.dram_tensor("in_" + k, a.shape, mybir.dt.from_np(a.dtype), kind="ExternalInput").ap() for k, a in arrays.items()}
    t["out"] = nc.dram_tensor("out", (B, S, D), F32, kind="ExternalOutput").ap()
    build(nc, t)
    arrays = {"in_" + k: a for k, a in arrays.items()}
    return run_bass_kernel_spmd(nc, [arrays], core_ids=[0]).results[0]["out"]
```
